# Optimizing a Trainium2 kernel written in Bass

```python
import numpy as np
import jax
import jax.numpy as jnp

def _softmax(x, axis=-1):
    return jax.nn.softmax(x, axis=axis)
def _gelu(x):
    return jax.nn.gelu(x, approximate=True)
def _silu(x):
    return jax.nn.silu(x)
def _sigmoid(x):
    return jax.nn.sigmoid(x)
def _layernorm(x, axis=-1, eps=1e-5):
    m = jnp.mean(x, axis=axis, keepdims=True)
    v = jnp.var(x, axis=axis, keepdims=True)
    return (x - m) / jnp.sqrt(v + eps)
def _scatter_add(tgt, idx, src, axis=0):
    return tgt.at[idx].add(src)
def _segment_sum(src, seg, n):
    return jax.ops.segment_sum(src, seg, n)

kernel_name = 'mk_conv_seq_d1_conv_nchw64_949f32'

def setup_inputs(seed: int = 0):
    np.random.seed(seed)
    _w = jnp.asarray
    def _rec_inputs():
        import jax
        import jax.numpy as jnp
        _gk = jax.random.key(seed)
        x = -0.0001272 + 0.9999 * jax.random.normal(jax.random.fold_in(_gk, 1), (8, 64, 161, 400), jnp.float32)
        return x
    x = _rec_inputs()
    def _L0_conv_setup():
        import jax, jax.numpy as jnp
        import numpy as np
        B, C, F, T = (8, 64, 161, 400)
        H, N2 = (161, 32)

        def _layernorm(x, w, b):
            mean = x.mean(axis=(1, 2), keepdims=True)
            std = jnp.sqrt(x.var(axis=(1, 2), ddof=1, keepdims=True))
            return (x - mean) / (std + 1e-08) * w + b

        def _conv2d(x, w, b, pad_h):
            y = jax.lax.conv_general_dilated(x, w, window_strides=(1, 1), padding=((pad_h, pad_h), (0, 0)), dimension_numbers=('NCHW', 'OIHW', 'NCHW'))
            return y + b[None, :, None, None]

        def _s4d(u, log_dt, log_A_real, A_imag, C_re, C_im, Dskip, Wout, bout):
            u = jnp.swapaxes(u, 1, 2)
            L = u.shape[-1]
            dt = jnp.exp(log_dt)[:, None]
            A = -jnp.exp(log_A_real) + 1j * A_imag
            dtA = A * dt
            Cbar = (C_re + 1j * C_im) * (jnp.exp(dtA) - 1.0) / A
            vand = jnp.exp(dtA[:, :, None] * jnp.arange(L, dtype=jnp.float32))
            K = 2.0 * jnp.einsum('hn,hnl->hl', Cbar, vand).real
            kf = jnp.fft.rfft(K, n=2 * L)
            uf = jnp.fft.rfft(u, n=2 * L)
            y = jnp.fft.irfft(uf * kf, n=2 * L)[..., :L]
            y = y + u * Dskip[:, None]
            y = jax.nn.gelu(y, approximate=False)
            y = jnp.einsum('ch,bhl->bcl', Wout, y) + bout[None, :, None]
            y = y[:, :H] * jax.nn.sigmoid(y[:, H:])
            return jnp.swapaxes(y, 1, 2)
        key = jax.random.key(seed)
        ks = jax.random.split(key, 16)
        x = jax.random.normal(ks[0], (B, C, F, T), jnp.float32)
        log_dt = jax.random.uniform(ks[1], (H,)) * (np.log(0.1) - np.log(0.001)) + np.log(0.001)
        log_A_real = jnp.log(0.5 * jnp.ones((H, N2), jnp.float32))
        A_imag = np.pi * jnp.tile(jnp.arange(N2, dtype=jnp.float32)[None, :], (H, 1))
        C_re = jax.random.normal(ks[2], (H, N2)) * 0.5 ** 0.5
        C_im = jax.random.normal(ks[3], (H, N2)) * 0.5 ** 0.5
        Dskip = jax.random.normal(ks[4], (H,))
        Wout = jax.random.normal(ks[5], (2 * H, H)) * (1.0 / np.sqrt(H))
        bout = jnp.zeros((2 * H,), jnp.float32)
        w0 = jnp.ones((1, C, F, 1), jnp.float32)
        b0 = jax.random.uniform(ks[6], (1, C, F, 1)) * 0.0001
        w1 = jnp.ones((1, C, F, 1), jnp.float32)
        b1 = jax.random.uniform(ks[7], (1, C, F, 1)) * 0.0001
        Wg = jax.random.normal(ks[8], (C, C, 1, 1)) * (1.0 / np.sqrt(C))
        bg = jnp.zeros((C,), jnp.float32)
        Wi = jax.random.normal(ks[9], (C, C, 1, 1)) * (1.0 / np.sqrt(C))
        bi = jnp.zeros((C,), jnp.float32)
        Wc = jax.random.normal(ks[10], (C, C, 3, 1)) * (1.0 / np.sqrt(3 * C))
        bc = jnp.zeros((C,), jnp.float32)
        return dict(x=x, log_dt=log_dt, log_A_real=log_A_real, A_imag=A_imag, C_re=C_re, C_im=C_im, Dskip=Dskip, Wout=Wout, bout=bout, w0=w0, b0=b0, w1=w1, b1=b1, Wg=Wg, bg=bg, Wi=Wi, bi=bi, Wc=Wc, bc=bc)
    _L0_conv_all = _L0_conv_setup()
    _L0_conv_in = {k: v for k, v in _L0_conv_all.items() if k in ('log_dt', 'log_A_real', 'A_imag', 'C_re', 'C_im', 'Dskip', 'Wout', 'bout', 'w0', 'b0', 'w1', 'b1', 'Wg', 'bg', 'Wi', 'bi', 'Wc', 'bc', )}
    del _L0_conv_all

    return {
        "x": x,
        "L0_conv_log_dt": _L0_conv_in["log_dt"],
        "L0_conv_log_A_real": _L0_conv_in["log_A_real"],
        "L0_conv_A_imag": _L0_conv_in["A_imag"],
        "L0_conv_C_re": _L0_conv_in["C_re"],
        "L0_conv_C_im": _L0_conv_in["C_im"],
        "L0_conv_Dskip": _L0_conv_in["Dskip"],
        "L0_conv_Wout": _L0_conv_in["Wout"],
        "L0_conv_bout": _L0_conv_in["bout"],
        "L0_conv_w0": _L0_conv_in["w0"],
        "L0_conv_b0": _L0_conv_in["b0"],
        "L0_conv_w1": _L0_conv_in["w1"],
        "L0_conv_b1": _L0_conv_in["b1"],
        "L0_conv_Wg": _L0_conv_in["Wg"],
        "L0_conv_bg": _L0_conv_in["bg"],
        "L0_conv_Wi": _L0_conv_in["Wi"],
        "L0_conv_bi": _L0_conv_in["bi"],
        "L0_conv_Wc": _L0_conv_in["Wc"],
        "L0_conv_bc": _L0_conv_in["bc"],
    }

def reference(x, L0_conv_log_dt, L0_conv_log_A_real, L0_conv_A_imag, L0_conv_C_re, L0_conv_C_im, L0_conv_Dskip, L0_conv_Wout, L0_conv_bout, L0_conv_w0, L0_conv_b0, L0_conv_w1, L0_conv_b1, L0_conv_Wg, L0_conv_bg, L0_conv_Wi, L0_conv_bi, L0_conv_Wc, L0_conv_bc):
    import jax
    import jax.numpy as jnp
    def _L0_conv_ref(x, log_dt, log_A_real, A_imag, C_re, C_im, Dskip, Wout, bout, w0, b0, w1, b1, Wg, bg, Wi, bi, Wc, bc):
        import jax, jax.numpy as jnp
        import numpy as np
        B, C, F, T = (8, 64, 161, 400)
        H, N2 = (161, 32)

        def _layernorm(x, w, b):
            mean = x.mean(axis=(1, 2), keepdims=True)
            std = jnp.sqrt(x.var(axis=(1, 2), ddof=1, keepdims=True))
            return (x - mean) / (std + 1e-08) * w + b

        def _conv2d(x, w, b, pad_h):
            y = jax.lax.conv_general_dilated(x, w, window_strides=(1, 1), padding=((pad_h, pad_h), (0, 0)), dimension_numbers=('NCHW', 'OIHW', 'NCHW'))
            return y + b[None, :, None, None]

        def _s4d(u, log_dt, log_A_real, A_imag, C_re, C_im, Dskip, Wout, bout):
            u = jnp.swapaxes(u, 1, 2)
            L = u.shape[-1]
            dt = jnp.exp(log_dt)[:, None]
            A = -jnp.exp(log_A_real) + 1j * A_imag
            dtA = A * dt
            Cbar = (C_re + 1j * C_im) * (jnp.exp(dtA) - 1.0) / A
            vand = jnp.exp(dtA[:, :, None] * jnp.arange(L, dtype=jnp.float32))
            K = 2.0 * jnp.einsum('hn,hnl->hl', Cbar, vand).real
            kf = jnp.fft.rfft(K, n=2 * L)
            uf = jnp.fft.rfft(u, n=2 * L)
            y = jnp.fft.irfft(uf * kf, n=2 * L)[..., :L]
            y = y + u * Dskip[:, None]
            y = jax.nn.gelu(y, approximate=False)
            y = jnp.einsum('ch,bhl->bcl', Wout, y) + bout[None, :, None]
            y = y[:, :H] * jax.nn.sigmoid(y[:, H:])
            return jnp.swapaxes(y, 1, 2)
        b, c, f, t = x.shape
        u = x.transpose(0, 3, 1, 2).reshape(b * t, c, f)
        y = _s4d(u, log_dt, log_A_real, A_imag, C_re, C_im, Dskip, Wout, bout)
        x = y.reshape(b, t, c, f).transpose(0, 2, 3, 1) + x
        g = jax.nn.sigmoid(_conv2d(_layernorm(x, w0, b0), Wg, bg, 0))
        x = _conv2d(x, Wi, bi, 0)
        y = _conv2d(_layernorm(x * g, w1, b1), Wc, bc, 1)
        return y

    def _gn(v, G=32, eps=1e-5):
        B_, C_, H_, W_ = v.shape
        g = v.reshape(B_, G, C_ // G, H_, W_)
        m = jnp.mean(g, axis=(2, 3, 4), keepdims=True)
        s = jnp.var(g, axis=(2, 3, 4), keepdims=True)
        return ((g - m) / jnp.sqrt(s + eps)).reshape(v.shape)

    def _ln_c(v, eps=1e-6):
        m = jnp.mean(v, axis=1, keepdims=True)
        s = jnp.var(v, axis=1, keepdims=True)
        return (v - m) / jnp.sqrt(s + eps)

    def _ln_t(v, eps=1e-5):
        m = jnp.mean(v, axis=-1, keepdims=True)
        s = jnp.var(v, axis=-1, keepdims=True)
        return (v - m) / jnp.sqrt(s + eps)

    def _to_tokens(v):
        B_, C_, H_, W_ = v.shape
        return v.reshape(B_, C_, H_ * W_).transpose(0, 2, 1)
    def _from_tokens(t, like):
        B_, C_, H_, W_ = like.shape
        return t.transpose(0, 2, 1).reshape(B_, C_, H_, W_)

    x = _L0_conv_ref(x, L0_conv_log_dt, L0_conv_log_A_real, L0_conv_A_imag, L0_conv_C_re, L0_conv_C_im, L0_conv_Dskip, L0_conv_Wout, L0_conv_bout, L0_conv_w0, L0_conv_b0, L0_conv_w1, L0_conv_b1, L0_conv_Wg, L0_conv_bg, L0_conv_Wi, L0_conv_bi, L0_conv_Wc, L0_conv_bc)
    return x


_drawn_inputs = setup_inputs


def setup_inputs(seed=0):
    import zlib

    import numpy as np

    out = dict(_drawn_inputs(seed))
    spreads = {'L0_conv_log_A_real': (-0.6931471824645996, 0.6),
     'L0_conv_bout': (0.0, 0.1),
     'L0_conv_w0': (1.0, 0.2),
     'L0_conv_w1': (1.0, 0.2),
     'L0_conv_bg': (0.0, 0.1),
     'L0_conv_bi': (0.0, 0.1),
     'L0_conv_bc': (0.0, 0.1)}
    factors = {'L0_conv_b0': 8.0, 'L0_conv_b1': 8.0}
    for name, (base, spread) in spreads.items():
        noise = np.random.default_rng([zlib.crc32(name.encode()), seed]).standard_normal(out[name].shape)
        drawn = base * np.exp(spread * noise) if base else spread * noise
        out[name] = jnp.asarray(drawn.astype(out[name].dtype))
    for name, factor in factors.items():
        out[name] = (out[name] * factor).astype(out[name].dtype)
    return out
```

```python
from contextlib import ExitStack

import concourse.bass as bass
from concourse import mybir

F32 = mybir.dt.float32
F32R = mybir.dt.float32r
BF16 = mybir.dt.bfloat16
ACT = mybir.ActivationFunctionType
ALU = mybir.AluOpType
AX = mybir.AxisListType

P = 128
B, C, F, T = 8, 64, 161, 400
NS = 32
PAIRS = (F + 1) // 2
GP = 4
NG = -(-PAIRS // GP)
PER_B = T // P
TAIL = T - PER_B * P
NCHUNK = B * PER_B
XSLOTS = 7
OSLOTS = 3
H0 = 128
HR = F - H0
KR = 3 * HR + 2
LG = 4
NLG = C // LG
NSUB = C // 2
O2 = 2 * F
NTOT = C * F
SPLITS = [(0, 0), (0, 1), (0, 2), (1, 0), (1, 1), (2, 0)]
NSP = len(SPLITS)
K_MEAN, K_STD, K_ONE = 0, NSP, 2 * NSP
WIN = P - 32
LN1, LN2 = 10, 5
LN = LN1 + LN2
NLAG = 5
TWO_PI = 6.283185307179586
assert TAIL * B == P and NG % XSLOTS == 0 and NG % OSLOTS == 0


def pairs_of(g):
    return min(GP, PAIRS - g * GP)


def freqs_of(g):
    return min(2 * GP, F - g * 2 * GP)


def conv_seq_program(nc, x, log_dt, log_A_real, A_imag, C_re, C_im, Dskip, Wout, bout, w0, b0, w1, b1,
                     Wg, bg, Wi, bi, Wc, bc, out):
    ctx = ExitStack()
    with ctx:
        def sb(name, shape, dt=F32):
            return ctx.enter_context(nc.sbuf_tensor(name, shape, dt))

        def sem(name):
            return ctx.enter_context(nc.semaphore(name))

        xring = sb("xring", [P, XSLOTS, GP, P])
        toep = sb("toep", [P, PAIRS, C])
        tring = sb("tring", [P, 3, GP, P])
        z = sb("z", [P, C, F])
        x1 = sb("x1", [P, 2 * PAIRS, C])
        zh = sb("zh", [P, 2, LG, P], F32R)
        zl = sb("zl", [P, 2, LG, P], F32R)
        zr = sb("zr", [P, 2, LG, KR])
        zrT = sb("zrT", [P, 2, LG, P], F32R)
        turn = sb("turn", [P, 2, 3 * GP * P])
        sig = turn[:, 0, 0:4 * F].rearrange("p (s c f) -> p s c f", s=2, c=2)
        glu = turn[:, 0, 4 * F:8 * F].rearrange("p (s c f) -> p s c f", s=2, c=2)
        x1c = turn[:, 0, :].rearrange("p (s n t) -> p s n t", s=3, n=GP)
        gate = turn[:, 1, 0:2 * GP * P].rearrange("p (s w) -> p s w", s=2)
        vT = turn[:, 0, :].rearrange("p (s n t) -> p s n t", s=3, n=GP)
        oring = turn[:, 1, :].rearrange("p (s n t) -> p s n t", s=OSLOTS, n=GP)
        stats = sb("stats", [P, NSUB, 6])
        mv = sb("mv", [P, 2])
        ms = sb("ms", [P, 2])
        res = sb("res", [P, 2])
        rstd = sb("rstd", [P, 1])
        nmr = sb("nmr", [P, 1])
        var_n = sb("var_n", [P, 1])
        std = sb("std", [P, 1])
        half = sb("half", [P, 1])
        Lsrc = sb("Lsrc", [P, 224], BF16)
        Lt = sb("Lt", [P, 4, P], BF16)
        G = sb("G", [P, PAIRS, P])
        Wib = sb("Wib", [P, P])
        Wh = sb("Wh", [P, O2], F32R)
        Wl = sb("Wl", [P, O2], F32R)
        Wr = sb("Wr", [KR, O2], F32R)
        Wself = sb("Wself", [P, P])
        Wprev = sb("Wprev", [P, P])
        Rg = sb("Rg", [P, (NG // 4) * GP * P + P * pairs_of(NG - 1)], BF16)
        Rw = sb("Rw", [P, GP * P], BF16)
        w1c = sb("w1c", [P, PAIRS])
        obias = sb("obias", [P, PAIRS])
        ident = sb("ident", [P, P])
        identb = sb("identb", [P, P], BF16)

        ps = ctx.enter_context(nc.psum_tensor("ps", [P, 8, 512], F32))

        zf = z[:, :, :].rearrange("p a b -> p (a b)")
        xf = x1[:, :, :].rearrange("p a b -> p (a b)")
        used = {"x": 0, "z": 0}

        def scratch(where, a, b=None):
            n = a * (b or 1)
            at = used[where]
            used[where] += n
            assert used[where] <= C * F
            piece = (xf if where == "x" else zf)[:, at:at + n]
            return piece.rearrange("p (a b) -> p a b", a=a) if b else piece

        Qr = scratch("z", 2 * C, NS).rearrange("p (a l) n -> p a l n", a=2)
        Qi = scratch("z", 2 * C, NS).rearrange("p (a l) n -> p a l n", a=2)
        tsb = zf[:, 0:2 * C * C].rearrange("p (a j l) -> p a j l", a=2, j=C)
        Ta = scratch("x", C, NS).rearrange("p (a l) n -> p a l n", a=2)
        Tb = scratch("x", C, NS).rearrange("p (a l) n -> p a l n", a=2)
        ldt, dsk, dt_ = (scratch("x", 2) for _ in range(3))
        lAr, Aim, Cr, Ci, eA, ah, bb, kf, ang, th, sn, sh = (scratch("x", 2, NS) for _ in range(12))
        cs, em, ea, wr, wi, t1, t2, t3 = (scratch("x", 2, NS) for _ in range(8))
        kpad = scratch("x", 2, P)
        wraw = [scratch("x", F + 1) for _ in range(4)]
        w0c, b0c, b1c = (scratch("x", PAIRS) for _ in range(3))
        WgL, WiL, WgT = scratch("x", P), scratch("x", P), scratch("x", C)
        WcL, WcT = scratch("x", 6 * C), scratch("x", 3, C)
        WoL, WoR, boL, bc2 = scratch("x", 3, F), scratch("x", 3, KR), scratch("x", 3), scratch("x", 1)
        Gb = scratch("z", GP, P)
        mA, mB, mI = scratch("z", P + WIN), scratch("z", P + WIN), scratch("z", P)
        one1 = scratch("z", 2)
        bg1, bi1 = scratch("x", C), scratch("x", C)
        bgrow, birow = scratch("x", 2 * GP, C), scratch("x", 2 * GP, C)
        pmask = scratch("x", 3, P)
        pm = scratch("x", 3)
        sa, sb_, sc = (vT[:, i, :, :].rearrange("p a b -> p (a b)") for i in range(3))
        hb = [gate[:, 0, 0:256].bitcast(BF16), gate[:, 0, 256:512].bitcast(BF16), gate[:, 1, 0:256].bitcast(BF16)]
        kdram = nc.dram_tensor("kdram", [F, C * C], F32, kind="Internal").ap()

        s_par = sem("s_par")
        s_wts = sem("s_wts")
        s_kd = sem("s_kd")
        s_toep = sem("s_toep")
        s_zero = sem("s_zero")
        s_exp = sem("s_exp")
        s_arg = sem("s_arg")
        s_trig = sem("s_trig")
        s_kpad = sem("s_kpad")
        s_set = sem("s_set")
        s_pset = sem("s_pset")
        s_rows = sem("s_rows")
        s_wT = sem("s_wT")
        s_gb = sem("s_gb")
        s_gbu = sem("s_gbu")
        s_rg = sem("s_rg")
        s_rgev = sem("s_rgev")
        s_ob = sem("s_ob")
        s_ready = sem("s_ready")
        s_x = [sem(f"s_x{i}") for i in range(XSLOTS)]
        s_t = sem("s_t")
        s_conv = sem("s_conv")
        s_xt = sem("s_xt")
        s_gelu = sem("s_gelu")
        s_xtev = sem("s_xtev")
        s_zhi = sem("s_zhi")
        s_zr = sem("s_zr")
        s_zT = sem("s_zT")
        s_rT = sem("s_rT")
        s_zh = sem("s_zh")
        s_zrT = sem("s_zrT")
        s_zl = sem("s_zl")
        s_y = sem("s_y")
        s_sig = sem("s_sig")
        s_glu = sem("s_glu")
        s_add = sem("s_add")
        s_bn1 = sem("s_bn1")
        s_ln = sem("s_ln")
        s_std = sem("s_std")
        s_LT = sem("s_LT")
        s_Lt = sem("s_Lt")
        s_x1T = sem("s_x1T")
        s_x1c = sem("s_x1c")
        s_gw = sem("s_gw")
        s_gate = sem("s_gate")
        s_v = sem("s_v")
        s_bn2 = sem("s_bn2")
        s_n = sem("s_n")
        s_vT = sem("s_vT")
        s_vw = sem("s_vw")
        s_o = sem("s_o")
        s_oev = sem("s_oev")
        s_st = [sem(f"s_st{i}") for i in range(OSLOTS)]
        OEV = 1

        block = ctx.enter_context(nc.Block())

        def x_landed(j, g, tail):
            slot = g % XSLOTS
            dmas = [(freqs_of(i) if tail else min(2, freqs_of(i))) for i in range(slot, g + 1, XSLOTS)]
            a_chunk = sum(min(2, freqs_of(i)) for i in range(slot, NG, XSLOTS))
            return j * (16 * a_chunk) + 16 * sum(dmas)

        def out_halves(g):
            q0, n = g * GP, pairs_of(g)
            return [(max(q0, 1), n - (q0 == 0)), (q0, n)]

        def stored(j, groups, slot, tail):
            a_chunk = 32 * (NG // OSLOTS)
            mine = [sum(n for _, n in out_halves(i)) if tail else 2 for i in range(slot, NG, OSLOTS)]
            return j * a_chunk + OEV + 16 * sum(mine[:groups])

        @block.sync
        def _(sp):
            def halves(dst, src):
                sp.dma_start(dst[:, 0, :], src[0:P, :]).then_inc(s_par, 16)
                sp.dma_start(dst[0:HR, 1, :], src[P:F, :]).then_inc(s_par, 16)

            sp.wait_ge(s_zero, 1)
            for dst, src in ((lAr, log_A_real), (Aim, A_imag), (Cr, C_re), (Ci, C_im)):
                halves(dst, src)
            for dst, src in ((ldt, log_dt), (dsk, Dskip)):
                col = src.rearrange("(h a) -> h a", a=1)
                sp.dma_start(dst[:, 0:1], col[0:P, :]).then_inc(s_par, 16)
                sp.dma_start(dst[0:HR, 1:2], col[P:F, :]).then_inc(s_par, 16)
            for dst, src in ((WgL, Wg), (WiL, Wi)):
                for h in range(2):
                    sp.dma_start(dst[0:C, C * h:C * h + C], src[:, :, 0, 0]).then_inc(s_wts, 16)
            for h in range(2):
                sp.dma_start(WcL[0:C, 3 * C * h:3 * C * h + 3 * C],
                             Wc.rearrange("o c k a -> o (c k a)")).then_inc(s_wts, 16)
            for i in range(3):
                n = min(P, O2 - i * P)
                sp.dma_start(WoL[0:n, i, :], Wout[i * P:i * P + n, :]).then_inc(s_wts, 16)
                sp.dma_start(boL[0:n, i:i + 1], bout.rearrange("(h a) -> h a", a=1)[i * P:i * P + n, :])\
                  .then_inc(s_wts, 16)
            for dst, src in zip(wraw, (w0, b0, w1, b1)):
                for h in range(2):
                    sp.dma_start(dst[64 * h:64 * h + 64, 0:F], src[0, :, :, 0]).then_inc(s_wts, 16)
            for h in range(2):
                sp.dma_start(bc2[64 * h:64 * h + 64, :], bc.rearrange("(h a) -> h a", a=1)).then_inc(s_wts, 16)
            for row, src in ((bg1, bg), (bi1, bi)):
                sp.dma_start(row[0:1, :], src.rearrange("(a h) -> a h", a=1)).then_inc(s_wts, 16)

            def load_x(b, k, g):
                sp.wait_ge(s_xt, NG * (b * PER_B + k) + g + 1)
                for h in range(2):
                    m = (freqs_of(g) + 1 - h) // 2
                    if m:
                        src = bass.AP(x.tensor, b * (C * F * T) + k * P + (2 * GP * g + h) * T,
                                      [[F * T, C], [2 * T, m], [1, P]])
                        sp.dma_start(xring[64 * h:64 * h + 64, g % XSLOTS, 0:m, :], src)\
                          .then_inc(s_x[g % XSLOTS], 16)

            def load_tail(g):
                sp.wait_ge(s_xt, NG * NCHUNK + g + 1)
                for i in range(freqs_of(g)):
                    src = bass.AP(x.tensor, (2 * GP * g + i) * T + PER_B * P,
                                  [[F * T, C], [C * F * T, B], [1, TAIL]])
                    dst = xring[64 * (i % 2):64 * (i % 2) + 64, g % XSLOTS, i // 2, :]
                    sp.dma_start(dst.rearrange("c (b t) -> c b t", b=B), src).then_inc(s_x[g % XSLOTS], 16)

            sp.wait_ge(s_kpad, 1)
            sp.dma_start(kdram[0:P, :], tsb[:, 0, :, :].rearrange("p j l -> p (j l)")).then_inc(s_kd, 16)
            sp.dma_start(kdram[P:F, :], tsb[0:HR, 1, :, :].rearrange("p j l -> p (j l)")).then_inc(s_kd, 16)
            sp.wait_ge(s_kd, 32)
            for h in range(2):
                n = PAIRS - h
                sp.dma_start(toep[64 * h:64 * h + 64, 0:n, :],
                             bass.AP(kdram.tensor, h * C * C, [[C, C], [2 * C * C, n], [1, C]]))\
                  .then_inc(s_toep, 16)

            with sp.Fori(0, B) as b:
                with sp.Fori(0, PER_B) as k:
                    for g in range(NG):
                        load_x(b, k, g)
            for g in range(NG):
                load_tail(g)
            for s in range(OSLOTS):
                sp.wait_ge(s_st[s], stored(NCHUNK, NG // OSLOTS, s, True))

        @block.gpsimd
        def _(pool):
            done = [0]

            def step(ins):
                done[0] += 1
                ins.then_inc(s_pset, 1)
                pool.wait_ge(s_pset, done[0])

            step(pool.memset(ident[:, :], 0.0))
            step(pool.affine_select(out=ident[:, :], in_=ident[:, :], compare_op=ALU.not_equal, fill=1.0,
                                    base=0, pattern=[[-1, P]], channel_multiplier=1))
            step(pool.tensor_copy(identb[:, :], ident[:, :]))
            step(pool.memset(half[:, :], 0.5))
            pool.wait_ge(s_ready, 1)

            def chunk(j):
                def low(i):
                    pool.wait_ge(s_zhi, NLG * j + i + 1)
                    pool.tensor_tensor(zr[:, i % 2, :, HR:2 * HR], z[:, LG * i:LG * i + LG, H0:F],
                                       zr[:, i % 2, :, 0:HR], ALU.subtract).then_inc(s_zr, 1)

                def add(s):
                    pool.wait_ge(s_glu, NSUB * j + s + 1)
                    dst = x1[:, 0:F, 2 * s:2 * s + 2]
                    pool.tensor_tensor(dst, dst, glu[:, s % 2, :, :].rearrange("p c f -> p f c"),
                                       ALU.add).then_inc(s_add, 1)

                low(0)
                low(1)
                for i in range(NLG):
                    if i + 2 < NLG:
                        low(i + 2)
                    add(2 * i)
                    add(2 * i + 1)
                for at in (0, LN1):
                    pool.wait_ge(s_ln, LN * j + at + 2)
                    pool.tensor_tensor(std[:, :], var_n[:, :], half[:, :], ALU.pow).then_inc(s_std, 1)

            with pool.Fori(0, NCHUNK + 1) as j:
                chunk(j)

        @block.scalar
        def _(act):
            act.wait_ge(s_par, 12 * 16)
            act.activation(dt_, ldt, ACT.Exp).then_inc(s_exp, 1)
            act.activation(eA, lAr, ACT.Exp).then_inc(s_exp, 1)
            act.wait_ge(s_arg, 1)
            act.activation(th, ah, ACT.Tanh).then_inc(s_trig, 1)
            act.activation(sn, ang, ACT.Sin).then_inc(s_trig, 1)
            act.activation(sh, ang, ACT.Sin, scale=0.5).then_inc(s_trig, 1)
            act.wait_ge(s_ready, 1)

            def chunk(j):
                for g in range(NG):
                    nf = freqs_of(g)
                    act.wait_ge(s_conv, NG * j + g + 1)
                    act.activation(z[:, :, 2 * GP * g:2 * GP * g + nf],
                                   ps[:, g % 2, 0:C * nf].rearrange("p (h l) -> p l h", h=nf),
                                   ACT.Gelu).then_inc(s_gelu, 1)
                    act.wait_ge(s_xt, NG * j + g + 1 + XSLOTS)
                    act.activation(xf[:, 2 * GP * C * g:2 * GP * C * g + C * nf], ps[:, 2 + g % 2, 0:C * nf],
                                   ACT.Copy).then_inc(s_xtev, 1)

                def sigmoid(s):
                    act.wait_ge(s_y, NSUB * j + s + 1)
                    if s >= 2:
                        act.wait_ge(s_glu, NSUB * j + s - 1)
                    bank = 4 + 2 * (s % 2)
                    act.activation(sig[:, s % 2, :, :], ps[:, bank:bank + 2, F:O2], ACT.Sigmoid).then_inc(s_sig, 1)

                def parts(i):
                    if i >= 2:
                        act.wait_ge(s_rT, NLG * j + i - 1)
                    src = z[:, LG * i:LG * i + LG, H0:F]
                    if i == 0:
                        act.wait_ge(s_gelu, NG * j + NG)
                    act.activation(zr[:, i % 2, :, 0:HR].bitcast(F32R), src, ACT.Copy)
                    act.activation(zr[:, i % 2, :, 2 * HR:3 * HR], src, ACT.Copy).then_inc(s_zhi, 1)

                parts(0)
                parts(1)
                for i in range(NLG + 1):
                    if i < NLG:
                        act.wait_ge(s_zT, NLG * j + i + 1)
                        if i >= 2:
                            act.wait_ge(s_y, NSUB * j + 2 * i - 2)
                        act.activation(zh[:, i % 2, :, :], ps[:, i % 2, :].rearrange("p (l t) -> p l t", l=LG),
                                       ACT.Copy).then_inc(s_zh, 1)
                        act.wait_ge(s_rT, NLG * j + i + 1)
                        act.activation(zrT[0:KR, i % 2, :, :],
                                       ps[0:KR, 2 + i % 2, :].rearrange("p (l t) -> p l t", l=LG),
                                       ACT.Copy).then_inc(s_zrT, 1)
                        if i + 2 < NLG:
                            parts(i + 2)
                    if i >= 1:
                        sigmoid(2 * i - 2)
                        sigmoid(2 * i - 1)
                for s in range(OSLOTS):
                    act.wait_ge(s_st[s], stored(j, 0, s, False))
                for g in range(NG + 2):
                    if g < NG:
                        n = pairs_of(g)
                        act.wait_ge(s_x1T, NG * j + g + 1)
                        if g >= 3:
                            act.wait_ge(s_gw, NG * j + g - 2)
                        act.activation(x1c[:, g % 3, 0:n, :],
                                       ps[:, g % 2, 0:P * n].rearrange("p (n t) -> p n t", n=n),
                                       ACT.Copy).then_inc(s_x1c, 1)
                    if g >= 2:
                        q = g - 2
                        w = C * freqs_of(q)
                        act.wait_ge(s_gw, NG * j + q + 1)
                        if q >= 2:
                            act.wait_ge(s_v, NG * j + q - 1)
                        act.activation(gate[:, q % 2, 0:w], ps[:, 4 + q % 2, 0:w], ACT.Sigmoid,
                                       scale=rstd[:, 0:1]).then_inc(s_gate, 1)

            def store(b, k, g):
                j = NCHUNK if b is None else b * PER_B + k
                act.wait_ge(s_oev, NG * j + g + 1 + OEV)
                for h, (q, n) in enumerate(out_halves(g)):
                    src = oring[64 * h:64 * h + 64, g % OSLOTS, q - GP * g:q - GP * g + n, :]
                    f0 = 2 * q - 1 + h
                    if b is not None:
                        dst = bass.AP(out.tensor, b * (C * F * T) + k * P + f0 * T, [[F * T, C], [2 * T, n], [1, P]])
                        act.dma_start(dst, src).then_inc(s_st[g % OSLOTS], 16)
                        continue
                    for i in range(n):
                        dst = bass.AP(out.tensor, (f0 + 2 * i) * T + PER_B * P,
                                      [[F * T, C], [C * F * T, B], [1, TAIL]])
                        act.dma_start(dst, src[:, i, :].rearrange("c (b t) -> c b t", b=B))\
                           .then_inc(s_st[g % OSLOTS], 16)

            def last_phase(b, k):
                j = NCHUNK if b is None else b * PER_B + k
                act.wait_ge(s_ln, LN * j + LN)
                for g in range(NG):
                    v = xf[:, 2 * GP * C * g:2 * GP * C * g + C * freqs_of(g)]
                    act.activation(v, v, ACT.Identity, scale=rstd[:, 0:1], bias=nmr[:, 0:1]).then_inc(s_n, 1)
                    if g >= NLAG:
                        store(b, k, g - NLAG)
                for g in range(NG - NLAG, NG):
                    store(b, k, g)

            with act.Fori(0, B) as b:
                with act.Fori(0, PER_B) as k:
                    chunk(b * PER_B + k)
                    last_phase(b, k)
            chunk(NCHUNK)
            last_phase(None, None)

        @block.tensor
        def _(pe):
            pe.wait_ge(s_pset, 4)
            pe.wait_ge(s_rows, 1)
            pe.transpose(ps[:, 0, 0:C], WgL[0:C, :], ident[0:C, 0:C])
            pe.transpose(ps[:, 0, C:2 * C], WiL[0:C, :], ident[0:C, 0:C])
            for k in range(3):
                pe.transpose(ps[:, 1, C * k:C * k + C], WcL[0:C, :].rearrange("o (c k) -> o k c", k=3)[:, k, :],
                             ident[0:C, 0:C])
            for i in range(3):
                n = min(P, O2 - i * P)
                pe.transpose(ps[:, 2, i * P:i * P + n], WoL[0:n, i, 0:H0], ident[0:n, 0:n])
                pe.transpose(ps[0:KR, 3, i * P:i * P + n], WoR[0:n, i, :], ident[0:n, 0:n])
            for i in range(3):
                pe.matmul(ps[:, 4, 2 * i:2 * i + 2], pmask[0:1, i, :], one1[0:1, :], start=True, stop=True)
            pe.matmul(ps[:, 5, :], mI[0:1, :], birow[0:1, :, :].rearrange("p a b -> p (a b)"), start=True,
                      stop=True).then_inc(s_wT, 1)
            for s in range(-(-NG // 4)):
                groups = range(4 * s, min(4 * s + 4, NG))
                if s >= 2:
                    pe.wait_ge(s_rgev, s - 1)
                for g in groups:
                    n = pairs_of(g)
                    o = ps[:, 6 + s % 2, 0:P * n]
                    at = WIN - 32 * (g % 4)
                    pe.wait_ge(s_gb, g + 1)
                    pe.matmul(o, mA[:, at:at + P], G[:, GP * g:GP * g + n, :].rearrange("p a b -> p (a b)"),
                              start=(g == groups[0]), stop=False, skip_group_check=True)
                    pe.matmul(o, mB[0:1, at:at + P], bgrow[0:1, 0:2 * n, :].rearrange("p a b -> p (a b)"),
                              start=False, stop=False, skip_group_check=True)
                    pe.matmul(o, mB[:, at:at + P], Gb[:, 0:n, :].rearrange("p a b -> p (a b)"),
                              start=False, stop=(g == groups[-1]), skip_group_check=True).then_inc(s_gbu, 1)
            pe.matmul(ps[:, 0, 0:PAIRS], Wself[:, :], b1c, start=True, stop=False, skip_group_check=True)
            pe.matmul(ps[:, 0, 1:PAIRS], Wprev[:, :], b1c[:, 0:PAIRS - 1], start=False, stop=True,
                      skip_group_check=True).then_inc(s_ob, 1)
            pe.wait_ge(s_ready, 1)

            def chunk(j, tail):
                for g in range(NG):
                    n = pairs_of(g)
                    pe.wait_ge(s_t, 2 * NG * j + 2 * g + 2)
                    pe.wait_ge(s_x[g % XSLOTS], x_landed(j, g, tail))
                    if g >= 2:
                        pe.wait_ge(s_gelu, NG * j + g - 1)
                    for i in range(n):
                        ins = pe.matmul(ps[:, g % 2, P * i:P * i + P], xring[:, g % XSLOTS, i, :],
                                        tring[:, g % 3, i, :], start=True, stop=True)
                    ins.then_inc(s_conv, 1)
                    if g >= 2:
                        pe.wait_ge(s_xtev, NG * j + g - 1)
                    for i in range(n):
                        ins = pe.transpose(ps[:, 2 + g % 2, P * i:P * i + P], xring[:, g % XSLOTS, i, :],
                                           ident[:, :])
                    ins.then_inc(s_xt, 1)
                pe.wait_ge(s_gelu, NG * j + NG)
                for i in range(NLG + 1):
                    if i < NLG:
                        if i >= 2:
                            pe.wait_ge(s_zl, NLG * j + i - 1)
                        for c in range(LG):
                            ins = pe.transpose(ps[:, i % 2, P * c:P * c + P], z[:, LG * i + c, 0:H0], ident[:, :])
                        ins.then_inc(s_zT, 1)
                        pe.wait_ge(s_zr, NLG * j + i + 1)
                        if i == 0:
                            pe.wait_ge(s_xtev, NG * j + NG)
                        if i >= 2:
                            pe.wait_ge(s_zrT, NLG * j + i - 1)
                        for c in range(LG):
                            ins = pe.transpose(ps[0:KR, 2 + i % 2, P * c:P * c + P], zr[:, i % 2, c, :],
                                               ident[:, :])
                        ins.then_inc(s_rT, 1)
                    if i >= 1:
                        k = (i - 1) % 2
                        pe.wait_ge(s_zrT, NLG * j + i)
                        pe.wait_ge(s_zl, NLG * j + i)
                        for s in (2 * i - 2, 2 * i - 1):
                            if s == 0:
                                pe.wait_ge(s_oev, NG * j + OEV)
                            if s >= 2:
                                pe.wait_ge(s_glu, NSUB * j + s - 1)
                            for c in range(2):
                                o = ps[:, 4 + 2 * (s % 2) + c, 0:O2]
                                l = 2 * (s % 2) + c
                                pe.matmul(o, zh[:, k, l, :], Wh[:, :], start=True, stop=False)
                                pe.matmul(o, zh[:, k, l, :], Wl[:, :], start=False, stop=False)
                                pe.matmul(o, zl[:, k, l, :], Wh[:, :], start=False, stop=False)
                                ins = pe.matmul(o, zrT[0:KR, k, l, :], Wr[:, :], start=False, stop=True)
                            ins.then_inc(s_y, 1)
                pe.wait_ge(s_add, NSUB * j + NSUB)
                for g in range(NG + 2):
                    if g < NG:
                        n = pairs_of(g)
                        if g >= 2:
                            pe.wait_ge(s_x1c, NG * j + g - 1)
                        for i in range(n):
                            f = 2 * (GP * g + i)
                            ins = pe.transpose(ps[:, g % 2, P * i:P * i + P], xf[:, C * f:C * f + P], ident[:, :])
                        ins.then_inc(s_x1T, 1)
                    if 1 <= g <= NG:
                        k = g - 1
                        n = pairs_of(k)
                        pe.wait_ge(s_x1c, NG * j + k + 1)
                        if k == 0:
                            pe.wait_ge(s_glu, NSUB * j + NSUB)
                        if k >= 2:
                            pe.wait_ge(s_v, NG * j + k - 1)
                        for i in range(n):
                            pe.matmul(ps[:, 4 + k % 2, P * i:P * i + P], x1c[:, k % 3, i, :], G[:, GP * k + i, :],
                                      start=(i == 0), stop=False, skip_group_check=True)
                            pe.matmul(ps[:, 6 + k % 2, P * i:P * i + P], x1c[:, k % 3, i, :], Wib[:, :],
                                      start=(i == 0), stop=False, skip_group_check=True)
                    if g >= 2:
                        k = g - 2
                        if k == 0:
                            pe.wait_ge(s_ln, LN * j + LN1)
                            for q in range(4):
                                at = WIN - 32 * q
                                ins = pe.transpose(ps[:, 2, 0:256].bitcast(BF16)[:, P * q:P * q + P],
                                                   Lsrc[:, at:at + P], identb[:, :])
                            ins.then_inc(s_LT, 1)
                            pe.wait_ge(s_Lt, j + 1)
                        w = P * pairs_of(k)
                        pe.matmul(ps[:, 4 + k % 2, 0:w], Lt[:, k % 4, :], Rg[:, GP * P * (k // 4):GP * P * (k // 4) + w],
                                  start=False, stop=True, skip_group_check=True)
                        pe.matmul(ps[:, 6 + k % 2, 0:w], Lt[:, 0, :], Rw[:, 0:w],
                                  start=False, stop=True, skip_group_check=True).then_inc(s_gw, 1)
                for g in range(NG + 1):
                    if g < NG:
                        n = pairs_of(g)
                        pe.wait_ge(s_n, NG * j + g + 1)
                        if g >= 2:
                            pe.wait_ge(s_vw, NG * j + g - 1)
                        for i in range(n):
                            f = 2 * (GP * g + i)
                            ins = pe.transpose(ps[:, g % 2, P * i:P * i + P], xf[:, C * f:C * f + P], ident[:, :])
                        ins.then_inc(s_vT, 1)
                    if g >= 1:
                        k = g - 1
                        n = pairs_of(k)
                        pe.wait_ge(s_vw, NG * j + k + 1)
                        if k >= 2:
                            pe.wait_ge(s_oev, NG * j + k - 1 + OEV)
                        o = ps[:, 4 + k % 2, :]
                        ins = pe.matmul(o[:, 0:P * n], Wself[:, :], vT[:, k % 3, 0:n, :].rearrange("p n t -> p (n t)"),
                                        start=True, stop=False, skip_group_check=True)
                        if k > 0:
                            ins = pe.matmul(o[:, 0:P], Wprev[:, :], vT[:, (k - 1) % 3, GP - 1, :],
                                            start=False, stop=(n == 1), skip_group_check=True)
                        if n > 1:
                            ins = pe.matmul(o[:, P:P * n], Wprev[:, :],
                                            vT[:, k % 3, 0:n - 1, :].rearrange("p n t -> p (n t)"),
                                            start=False, stop=True, skip_group_check=True)
                        ins.then_inc(s_o, 1)

            with pe.Fori(0, NCHUNK) as j:
                chunk(j, False)
            chunk(NCHUNK, True)

        @block.vector
        def _(dve):
            done = [0]

            def step(ins):
                done[0] += 1
                ins.then_inc(s_set, 1)
                dve.wait_ge(s_set, done[0])

            def tt(o, a, b, op):
                step(dve.tensor_tensor(o, a, b, op))

            def ts(o, a, s1, s2, op0, op1=ALU.bypass):
                step(dve.tensor_scalar(o, a, s1, s2, op0, op1) if s2 is not None
                     else dve.tensor_scalar(o, a, s1, None, op0))

            def stt(o, a, s, b, op0, op1):
                step(dve.scalar_tensor_tensor(out=o, in0=a, scalar=s, in1=b, op0=op0, op1=op1))

            add, sub, mul = ALU.add, ALU.subtract, ALU.mult
            dve.memset(xf, 0.0).then_inc(s_zero, 1)
            step(dve.memset(zf, 0.0))
            step(dve.memset(tring[:, :, :, :], 0.0))
            step(dve.memset(G[:, :, :], 0.0))
            step(dve.memset(toep[64:P, PAIRS - 1, :], 0.0))
            for m in (Wib, Wself, Wprev, Lsrc, w1c):
                step(dve.memset(m[:, :], 0.0))
            step(dve.memset(Lsrc[:, WIN + K_ONE:WIN + K_ONE + 3], 1.0))
            step(dve.memset(zr[:, :, :, 3 * HR:KR].rearrange("p a l k -> p (a l) k"), 1.0))
            step(dve.memset(mA[:, WIN + K_MEAN:WIN + K_MEAN + NSP], -1.0))
            step(dve.memset(mB[:, WIN + K_STD:WIN + K_STD + NSP], 1.0))
            step(dve.memset(mI[:, K_ONE:K_ONE + 3], 1.0))
            step(dve.memset(one1, 1.0))
            dve.memset(ms[:, :], 0.0).then_inc(s_xt, XSLOTS)
            dve.memset(rstd[:, :], 0.0).then_inc(s_oev, OEV)
            for s in s_st:
                dve.memset(res[:, :], 0.0).then_inc(s, OEV)
                dve.wait_ge(s, OEV)
            dve.wait_ge(s_oev, OEV)
            dve.wait_ge(s_zero, 1)
            for k, part in [(K_MEAN + i, r) for i, (_, r) in enumerate(SPLITS)]\
                    + [(K_STD + i, r) for i, (_, r) in enumerate(SPLITS)] + [(K_ONE + i, i) for i in range(3)]:
                step(dve.memset(pmask[0:1, part, :].rearrange("p (q k) -> p q k", q=4)[:, :, k], 1.0))

            dve.wait_ge(s_exp, 2)
            dtb = dt_.unsqueeze(2).to_broadcast([P, 2, NS])
            tt(t1, eA, dtb, mul)
            ts(ah, t1, -0.5, None, mul)
            tt(bb, Aim, dtb, mul)
            magic = 12582912.0
            ts(kf, bb, 1.0 / TWO_PI, magic, mul, add)
            ts(t1, kf, magic, None, sub)
            rest = TWO_PI
            c1 = 6.28125
            c2 = 0.0019350051879882812
            c3 = rest - c1 - c2
            stt(t2, t1, -c1, bb, mul, add)
            stt(t3, t1, -c2, t2, mul, add)
            stt(t2, t1, -c3, t3, mul, add)
            dve.tensor_scalar(ang, t2, 3.1415925, -3.1415925, ALU.min, ALU.max).then_inc(s_arg, 1)
            dve.wait_ge(s_trig, 3)
            tt(t1, sh, sh, mul)
            ts(t1, t1, -2.0, None, mul)
            ts(cs, t1, 1.0, None, add)
            ts(t2, th, -1.0, 1.0, mul, add)
            step(dve.reciprocal(t3, t2))
            tt(t2, th, t3, mul)
            ts(em, t2, 2.0, None, mul)
            ts(ea, em, 1.0, None, add)
            tt(wr, ea, cs, mul)
            tt(wi, ea, sn, mul)
            tt(t2, em, cs, mul)
            tt(em, t2, t1, add)
            ts(eA, eA, -1.0, None, mul)
            tt(t1, Cr, em, mul)
            tt(t2, Ci, wi, mul)
            tt(t3, t1, t2, sub)
            tt(t1, Cr, wi, mul)
            tt(t2, Ci, em, mul)
            tt(cs, t1, t2, add)
            tt(t1, eA, eA, mul)
            tt(t2, Aim, Aim, mul)
            tt(t1, t1, t2, add)
            step(dve.reciprocal(t2, t1))
            ts(t2, t2, 2.0, None, mul)
            tt(t1, t3, eA, mul)
            tt(ea, cs, Aim, mul)
            tt(t1, t1, ea, add)
            tt(Qr[:, :, 0, :], t1, t2, mul)
            tt(t1, cs, eA, mul)
            tt(ea, t3, Aim, mul)
            tt(t1, t1, ea, sub)
            tt(Qi[:, :, 0, :], t1, t2, mul)
            s = 1
            while s < C:
                wrb = wr.unsqueeze(2).to_broadcast([P, 2, s, NS])
                wib = wi.unsqueeze(2).to_broadcast([P, 2, s, NS])
                lo_r, lo_i, hi_r, hi_i = Qr[:, :, 0:s], Qi[:, :, 0:s], Qr[:, :, s:2 * s], Qi[:, :, s:2 * s]
                tt(Ta[:, :, 0:s], lo_r, wrb, mul)
                tt(Tb[:, :, 0:s], lo_i, wib, mul)
                tt(hi_r, Ta[:, :, 0:s], Tb[:, :, 0:s], sub)
                if 2 * s < C:
                    tt(Ta[:, :, 0:s], lo_r, wib, mul)
                    tt(Tb[:, :, 0:s], lo_i, wrb, mul)
                    tt(hi_i, Ta[:, :, 0:s], Tb[:, :, 0:s], add)
                    tt(t1, wr, wr, mul)
                    tt(t2, wi, wi, mul)
                    tt(t3, wr, wi, mul)
                    tt(wr, t1, t2, sub)
                    ts(wi, t3, 2.0, None, mul)
                s *= 2
            step(dve.tensor_reduce(kpad[:, :, C - 1:2 * C - 1], Qr, AX.X, add))
            k0 = kpad[:, :, C - 1]
            tt(k0, k0, dsk, add)
            for i in range(C):
                ins = dve.tensor_copy(tsb[:, :, i, :], kpad[:, :, C - 1 - i:2 * C - 1 - i])
            ins.then_inc(s_kpad, 1)

            dve.wait_ge(s_wts, 16 * 24)
            last = WoL[:, :, H0:F]
            step(dve.tensor_copy(WoR[:, :, 0:HR].bitcast(F32R), last))
            step(dve.tensor_copy(WoR[:, :, HR:2 * HR].bitcast(F32R), last))
            tt(WoR[:, :, 2 * HR:3 * HR], last, WoR[:, :, 0:HR], sub)
            step(dve.tensor_copy(WoR[:, :, 3 * HR].bitcast(F32R), boL))
            tt(WoR[:, :, 3 * HR + 1], boL, WoR[:, :, 3 * HR], sub)
            for row, src in ((bgrow, bg1), (birow, bi1)):
                step(dve.tensor_copy(row[0:1, :, :], src[0:1, :].unsqueeze(1).to_broadcast([1, 2 * GP, C])))
            for dst, src in zip((w0c, b0c, w1c[:, :], b1c), wraw):
                step(dve.tensor_copy(dst[0:C, :], src[0:C, 0:F:2]))
                step(dve.tensor_copy(dst[C:P, 0:PAIRS - 1], src[C:P, 1:F:2]))
            dve.memset(mv[:, :], 0.0).then_inc(s_rows, 1)
            dve.wait_ge(s_wT, 1)
            step(dve.tensor_copy(WgT, ps[:, 0, 0:C]))
            for h in range(2):
                r = slice(C * h, C * h + C)
                step(dve.tensor_copy(Wib[r, r], ps[r, 0, C:2 * C]))
                step(dve.tensor_copy(Wself[r, C:P], ps[r, 1, C * (1 + h):C * (2 + h)]))
                step(dve.tensor_copy(Wprev[r, 0:C], ps[r, 1, C * h:C * h + C]))
            step(dve.tensor_copy(Wself[0:C, 0:C], ps[0:C, 1, 2 * C:3 * C]))
            step(dve.tensor_copy(Wprev[C:P, C:P], ps[C:P, 1, 0:C]))
            step(dve.tensor_copy(Wh[:, :], ps[:, 2, 0:O2]))
            tt(Wl[:, :], ps[:, 2, 0:O2], Wh[:, :].bitcast(F32), sub)
            step(dve.tensor_copy(Wr[:, :], ps[0:KR, 3, 0:O2]))
            step(dve.tensor_copy(pm, ps[:, 4, 0:6:2]))
            for h in range(2):
                r = slice(C * h, C * h + C)
                tt(G[r, :, r], WgT[r, :].unsqueeze(1).to_broadcast([C, PAIRS, C]),
                   w0c[r, :].unsqueeze(2).to_broadcast([C, PAIRS, C]), mul)

            def split(bank, w, dst):
                src = ps[:, bank, 0:w]
                step(dve.tensor_copy(hb[0][:, 0:w], src))
                tt(sa[:, 0:w], src, hb[0][:, 0:w], sub)
                step(dve.tensor_copy(hb[1][:, 0:w], sa[:, 0:w]))
                tt(sb_[:, 0:w], sa[:, 0:w], hb[1][:, 0:w], sub)
                step(dve.tensor_copy(hb[2][:, 0:w], sb_[:, 0:w]))
                ts(sa[:, 0:w], hb[0][:, 0:w], pm[:, 0:1], None, mul)
                stt(sc[:, 0:w], hb[1][:, 0:w], pm[:, 1:2], sa[:, 0:w], mul, add)
                return dve.scalar_tensor_tensor(out=dst, in0=hb[2][:, 0:w], scalar=pm[:, 2:3], in1=sc[:, 0:w],
                                                op0=mul, op1=add)

            step(split(5, P * GP, Rw[:, :]))
            for g in range(NG):
                n = pairs_of(g)
                if g >= 1:
                    dve.wait_ge(s_gbu, g)
                for h in range(2):
                    r = slice(C * h, C * h + C)
                    ins = dve.tensor_tensor(Gb[r, 0:n, r], WgT[r, :].unsqueeze(1).to_broadcast([C, n, C]),
                                            b0c[r, GP * g:GP * g + n].unsqueeze(2).to_broadcast([C, n, C]), mul)
                    if h == 0:
                        step(ins)
                ins.then_inc(s_gb, 1)
                if g % 4 == 3 or g == NG - 1:
                    w = P * (GP if g % 4 == 3 else n)
                    dve.wait_ge(s_gbu, g + 1)
                    split(6 + (g // 4) % 2, w, Rg[:, GP * P * (g // 4):GP * P * (g // 4) + w]).then_inc(s_rgev, 1)
                    dve.wait_ge(s_rgev, g // 4 + 1)
            dve.wait_ge(s_ob, 1)
            ts(obias[:, :], ps[:, 0, 0:PAIRS], bc2, None, add)
            dve.memset(xf[:, C * F:], 0.0).then_inc(s_ready, 1)
            dve.wait_ge(s_ready, 1)
            dve.wait_ge(s_toep, 32)

            def chunk(j, tail):
                for g in range(NG):
                    n = pairs_of(g)
                    if g >= 3:
                        dve.wait_ge(s_conv, NG * j + g - 2)
                    for h in range(2):
                        dve.tensor_copy(tring[64 * h:64 * h + 64, g % 3, 0:n, 64 * h:64 * h + 64],
                                        toep[64 * h:64 * h + 64, GP * g:GP * g + n, :]).then_inc(s_t, 1)
                def bn1(s):
                    dve.wait_ge(s_add, NSUB * j + s + 1)
                    dve.bn_stats(stats[:, s, :], x1[:, 0:F, 2 * s:2 * s + 2]).then_inc(s_bn1, 1)

                for i in range(NLG + 1):
                    if i < NLG:
                        dve.wait_ge(s_zh, NLG * j + i + 1)
                        if i >= 2:
                            dve.wait_ge(s_y, NSUB * j + 2 * i - 2)
                        dve.tensor_tensor(zl[:, i % 2, :, :], ps[:, i % 2, :].rearrange("p (l t) -> p l t", l=LG),
                                          zh[:, i % 2, :, :].bitcast(F32), sub).then_inc(s_zl, 1)
                    if i >= 1:
                        for s in (2 * i - 2, 2 * i - 1):
                            dve.wait_ge(s_sig, NSUB * j + s + 1)
                            if s >= 2:
                                dve.wait_ge(s_add, NSUB * j + s - 1)
                            bank = 4 + 2 * (s % 2)
                            dve.tensor_tensor(glu[:, s % 2, :, :], ps[:, bank:bank + 2, 0:F], sig[:, s % 2, :, :],
                                              mul).then_inc(s_glu, 1)
                            if s >= 2:
                                bn1(s - 2)
                bn1(NSUB - 2)
                bn1(NSUB - 1)

                at = [LN * j]

                def ln_step(ins):
                    at[0] = at[0] + 1
                    ins.then_inc(s_ln, 1)
                    dve.wait_ge(s_ln, at[0])

                def std_of(nstats, roots):
                    ln_step(dve.bn_aggr(mv[:, :], stats[:, 0:nstats, :]))
                    ln_step(dve.tensor_scalar(var_n[:, :], mv[:, 1:2], float(NTOT) / (NTOT - 1), None, mul))
                    dve.wait_ge(s_std, roots)
                    ln_step(dve.tensor_scalar(ms[:, 1:2], std[:, :], 1e-8, None, add))
                    ln_step(dve.reciprocal(rstd[:, :], ms[:, 1:2]))

                dve.wait_ge(s_ready, 1)
                dve.wait_ge(s_bn1, NSUB * j + NSUB)
                std_of(NSUB, 2 * j + 1)
                ln_step(dve.tensor_copy(ms[:, 0:1], mv[:, 0:1]))
                fac = Lsrc[:, WIN:WIN + 2 * NSP].rearrange("p (m k) -> p m k", m=2)
                rest = ms[:, :]
                for part in range(3):
                    ks = [k for k, (lp, _) in enumerate(SPLITS) if lp == part]
                    ln_step(dve.tensor_copy(fac[:, :, ks[0]:ks[-1] + 1],
                                            rest.unsqueeze(2).to_broadcast([P, 2, len(ks)])))
                    if part < 2:
                        ln_step(dve.tensor_tensor(res[:, :], rest, fac[:, :, ks[0]], sub))
                        rest = res[:, :]
                dve.wait_ge(s_LT, j + 1)
                dve.tensor_copy(Lt[:, :, :].rearrange("p q t -> p (q t)"), ps[:, 2, 0:256].bitcast(BF16))\
                   .then_inc(s_Lt, 1)

                def bn2(g):
                    dve.wait_ge(s_v, NG * j + g + 1)
                    v = xf[:, 2 * GP * C * g:2 * GP * C * g + C * freqs_of(g)]
                    dve.bn_stats(stats[:, g, :], v).then_inc(s_bn2, 1)

                for g in range(NG):
                    w = C * freqs_of(g)
                    dve.wait_ge(s_gate, NG * j + g + 1)
                    dve.tensor_tensor(xf[:, 2 * GP * C * g:2 * GP * C * g + w], ps[:, 6 + g % 2, 0:w],
                                      gate[:, g % 2, 0:w], mul).then_inc(s_v, 1)
                    if g >= 1:
                        bn2(g - 1)
                bn2(NG - 1)
                dve.wait_ge(s_ready, 1)
                dve.wait_ge(s_bn2, NG * j + NG)
                std_of(NG, 2 * j + 2)
                ln_step(dve.tensor_scalar(nmr[:, :], mv[:, 0:1], rstd[:, 0:1], -1.0, mul, mul))

                for g in range(NG + 2):
                    if g < NG:
                        n = pairs_of(g)
                        dve.wait_ge(s_vT, NG * j + g + 1)
                        if g >= 3:
                            dve.wait_ge(s_o, NG * j + g - 1)
                        dve.tensor_tensor(vT[:, g % 3, 0:n, :], ps[:, g % 2, 0:P * n].rearrange("p (n t) -> p n t", n=n),
                                          w1c[:, GP * g:GP * g + n].unsqueeze(2).to_broadcast([P, n, P]),
                                          mul).then_inc(s_vw, 1)
                    if g >= 2:
                        q = g - 2
                        n = pairs_of(q)
                        dve.wait_ge(s_o, NG * j + q + 1)
                        dve.wait_ge(s_st[q % OSLOTS], stored(j, q // OSLOTS, q % OSLOTS, tail))
                        dve.tensor_tensor(oring[:, q % OSLOTS, 0:n, :],
                                          ps[:, 4 + q % 2, 0:P * n].rearrange("p (n t) -> p n t", n=n),
                                          obias[:, GP * q:GP * q + n].unsqueeze(2).to_broadcast([P, n, P]),
                                          add).then_inc(s_oev, 1)

            with dve.Fori(0, NCHUNK) as j:
                chunk(j, False)
            chunk(NCHUNK, True)


_NAMES = ["log_dt", "log_A_real", "A_imag", "C_re", "C_im", "Dskip", "Wout", "bout", "w0", "b0", "w1", "b1",
          "Wg", "bg", "Wi", "bi", "Wc", "bc"]


def kernel(**inputs):
    import numpy as _np
    import concourse.bacc as _bacc
    from concourse import mybir as _mybir
    from concourse.bass_utils import run_bass_kernel_spmd as _run

    nc = _bacc.Bacc("TRN2", target_bir_lowering=False, num_devices=1)
    arrays, args = {}, []
    for name in ["x"] + ["L0_conv_" + n for n in _NAMES]:
        a = _np.ascontiguousarray(inputs[name])
        arrays[f"in_{name}_dram"] = a
        args.append(nc.dram_tensor(f"in_{name}_dram", a.shape, _mybir.dt.from_np(a.dtype),
                                   kind="ExternalInput").ap())
    out = nc.dram_tensor("out_dram", (B, C, F, T), F32, kind="ExternalOutput").ap()
    conv_seq_program(nc, *args, out)
    r = _run(nc, [arrays], core_ids=[0])
    return r.results[0]["out_dram"]
```

```python
from contextlib import ExitStack

import concourse.bass as bass
from concourse import mybir

F32 = mybir.dt.float32
F32R = mybir.dt.float32r
BF16 = mybir.dt.bfloat16
ACT = mybir.ActivationFunctionType
ALU = mybir.AluOpType
AX = mybir.AxisListType

P = 128
B, C, F, T = 8, 64, 161, 400
NS = 32
PAIRS = (F + 1) // 2
GP = 4
NG = -(-PAIRS // GP)
PER_B = T // P
TAIL = T - PER_B * P
NCHUNK = B * PER_B
XSLOTS = 7
OSLOTS = 3
H0 = 128
HR = F - H0
KR = 3 * HR + 2
LG = 4
NLG = C // LG
NSUB = C // 2
O2 = 2 * F
NTOT = C * F
SPLITS = [(0, 0), (0, 1), (0, 2), (1, 0), (1, 1), (2, 0)]
NSP = len(SPLITS)
K_MEAN, K_STD, K_ONE = 0, NSP, 2 * NSP
WIN = P - 32
LN1, LN2 = 10, 5
LN = LN1 + LN2
EARLY = 6
VSLOTS = 4
SLAG = 4
TWO_PI = 6.283185307179586
assert TAIL * B == P and NG % XSLOTS == 0 and NG % OSLOTS == 0


def pairs_of(g):
    return min(GP, PAIRS - g * GP)


def freqs_of(g):
    return min(2 * GP, F - g * 2 * GP)


def conv_seq_program(nc, x, log_dt, log_A_real, A_imag, C_re, C_im, Dskip, Wout, bout, w0, b0, w1, b1,
                     Wg, bg, Wi, bi, Wc, bc, out):
    ctx = ExitStack()
    with ctx:
        def sb(name, shape, dt=F32):
            return ctx.enter_context(nc.sbuf_tensor(name, shape, dt))

        def sem(name):
            return ctx.enter_context(nc.semaphore(name))

        xring = sb("xring", [P, XSLOTS, GP, P])
        toep = sb("toep", [P, PAIRS, C])
        tring = sb("tring", [P, 3, GP, P])
        z = sb("z", [P, C, F])
        x1 = sb("x1", [P, 2 * PAIRS, C])
        parts = sb("parts", [P, 8, GP * P], F32R)

        def groups_in(at, n):
            return parts[:, at:at + n, :].rearrange("p s (i t) -> p s i t", i=GP)

        zh, zl = groups_in(0, 2), groups_in(2, 2)
        zrT = groups_in(4, 2)
        vh, vl = groups_in(0, VSLOTS), groups_in(VSLOTS, VSLOTS)
        turn = sb("turn", [P, 5 * GP * P])

        def piece(at, pattern, **sizes):
            n = 1
            for v in sizes.values():
                n *= v
            return turn[:, at:at + n].rearrange(pattern, **sizes)

        sig = piece(0, "p (s c f) -> p s c f", s=2, c=2, f=F)
        glu = piece(4 * F, "p (s c f) -> p s c f", s=2, c=2, f=F)
        zr = piece(8 * F, "p (s c k) -> p s c k", s=2, c=LG, k=KR)
        x1c = piece(0, "p (s n t) -> p s n t", s=2, n=GP, t=P)
        gate = piece(2 * GP * P, "p (s w) -> p s w", s=2, w=GP * P)
        oring = piece(0, "p (s n t) -> p s n t", s=OSLOTS, n=GP, t=P)
        vw = piece(3 * GP * P, "p (s n t) -> p s n t", s=2, n=GP, t=P)
        stats = sb("stats", [P, NSUB, 6])
        mv = sb("mv", [P, 2])
        ms = sb("ms", [P, 2])
        res = sb("res", [P, 2])
        rstd = sb("rstd", [P, 1])
        nmr = sb("nmr", [P, 1])
        var_n = sb("var_n", [P, 1])
        std = sb("std", [P, 1])
        half = sb("half", [P, 1])
        Lsrc = sb("Lsrc", [P, 224], BF16)
        Lt = sb("Lt", [P, 4, P], BF16)
        G = sb("G", [P, PAIRS, P])
        Wib = sb("Wib", [P, P])
        Wh = sb("Wh", [P, O2], F32R)
        Wl = sb("Wl", [P, O2], F32R)
        Wr = sb("Wr", [KR, O2], F32R)
        Wself, Wself_h, Wself_l = sb("Wself", [P, P]), sb("Wself_h", [P, P], F32R), sb("Wself_l", [P, P], F32R)
        Wprev, Wprev_h, Wprev_l = sb("Wprev", [P, P]), sb("Wprev_h", [P, P], F32R), sb("Wprev_l", [P, P], F32R)
        Rg = sb("Rg", [P, (NG // 4) * GP * P + P * pairs_of(NG - 1)], BF16)
        Rw = sb("Rw", [P, GP * P], BF16)
        w1c = sb("w1c", [P, PAIRS])
        obias = sb("obias", [P, PAIRS])
        ident = sb("ident", [P, P])
        identb = sb("identb", [P, P], BF16)

        ps = ctx.enter_context(nc.psum_tensor("ps", [P, 8, 512], F32))

        zf = z[:, :, :].rearrange("p a b -> p (a b)")
        xf = x1[:, :, :].rearrange("p a b -> p (a b)")
        used = {"x": 0, "z": 0}

        def scratch(where, a, b=None):
            n = a * (b or 1)
            at = used[where]
            used[where] += n
            assert used[where] <= C * F
            piece = (xf if where == "x" else zf)[:, at:at + n]
            return piece.rearrange("p (a b) -> p a b", a=a) if b else piece

        Qr = scratch("z", 2 * C, NS).rearrange("p (a l) n -> p a l n", a=2)
        Qi = scratch("z", 2 * C, NS).rearrange("p (a l) n -> p a l n", a=2)
        tsb = zf[:, 0:2 * C * C].rearrange("p (a j l) -> p a j l", a=2, j=C)
        Ta = scratch("x", C, NS).rearrange("p (a l) n -> p a l n", a=2)
        Tb = scratch("x", C, NS).rearrange("p (a l) n -> p a l n", a=2)
        ldt, dsk, dt_ = (scratch("x", 2) for _ in range(3))
        lAr, Aim, Cr, Ci, eA, ah, bb, kf, ang, th, sn, sh = (scratch("x", 2, NS) for _ in range(12))
        cs, em, ea, wr, wi, t1, t2, t3 = (scratch("x", 2, NS) for _ in range(8))
        kpad = scratch("x", 2, P)
        wraw = [scratch("x", F + 1) for _ in range(4)]
        w0c, b0c, b1c = (scratch("x", PAIRS) for _ in range(3))
        WgL, WiL, WgT = scratch("x", P), scratch("x", P), scratch("x", C)
        WcL, WcT = scratch("x", 6 * C), scratch("x", 3, C)
        WoL, WoR, boL, bc2 = scratch("x", 3, F), scratch("x", 3, KR), scratch("x", 3), scratch("x", 1)
        Gb = scratch("z", GP, P)
        mA, mB, mI = scratch("z", P + WIN), scratch("z", P + WIN), scratch("z", P)
        one1 = scratch("z", 2)
        bg1, bi1 = scratch("x", C), scratch("x", C)
        bgrow, birow = scratch("x", 2 * GP, C), scratch("x", 2 * GP, C)
        pmask = scratch("x", 3, P)
        pm = scratch("x", 3)
        sa, sb_, sc = (turn[:, GP * P * i:GP * P * (i + 1)] for i in range(3))
        hb = [turn[:, GP * P * 3 + 256 * i:GP * P * 3 + 256 * (i + 1)].bitcast(BF16) for i in range(3)]
        kdram = nc.dram_tensor("kdram", [F, C * C], F32, kind="Internal").ap()

        s_par = sem("s_par")
        s_wts = sem("s_wts")
        s_kd = sem("s_kd")
        s_toep = sem("s_toep")
        s_zero = sem("s_zero")
        s_exp = sem("s_exp")
        s_arg = sem("s_arg")
        s_trig = sem("s_trig")
        s_kpad = sem("s_kpad")
        s_set = sem("s_set")
        s_pset = sem("s_pset")
        s_rows = sem("s_rows")
        s_wT = sem("s_wT")
        s_gb = sem("s_gb")
        s_gbu = sem("s_gbu")
        s_rg = sem("s_rg")
        s_rgev = sem("s_rgev")
        s_ob = sem("s_ob")
        s_ready = sem("s_ready")
        s_x = [sem(f"s_x{i}") for i in range(XSLOTS)]
        s_t = sem("s_t")
        s_conv = sem("s_conv")
        s_xt = sem("s_xt")
        s_gelu = sem("s_gelu")
        s_xtev = sem("s_xtev")
        s_zhi = sem("s_zhi")
        s_zr = sem("s_zr")
        s_zT = sem("s_zT")
        s_rT = sem("s_rT")
        s_zh = sem("s_zh")
        s_zrT = sem("s_zrT")
        s_zl = sem("s_zl")
        s_y = sem("s_y")
        s_sig = sem("s_sig")
        s_glu = sem("s_glu")
        s_add = sem("s_add")
        s_bn1 = sem("s_bn1")
        s_ln = sem("s_ln")
        s_std = sem("s_std")
        s_LT = sem("s_LT")
        s_Lt = sem("s_Lt")
        s_x1T = sem("s_x1T")
        s_x1c = sem("s_x1c")
        s_gw = sem("s_gw")
        s_gate = sem("s_gate")
        s_v = sem("s_v")
        s_bn2 = sem("s_bn2")
        s_n = sem("s_n")
        s_vT = sem("s_vT")
        s_vw = sem("s_vw")
        s_vh = sem("s_vh")
        s_vl = sem("s_vl")
        s_one = sem("s_one")
        s_o = sem("s_o")
        s_oev = sem("s_oev")
        s_st = [sem(f"s_st{i}") for i in range(OSLOTS)]
        OEV = 1

        block = ctx.enter_context(nc.Block())

        def x_landed(j, g):
            slot = g % XSLOTS
            return j * (16 * sum(freqs_of(i) for i in range(slot, NG, XSLOTS))) \
                + 16 * sum(freqs_of(i) for i in range(slot, g + 1, XSLOTS))

        def out_halves(g):
            q0, n = g * GP, pairs_of(g)
            return [(max(q0, 1), n - (q0 == 0)), (q0, n)]

        def stored(j, groups, slot, tail):
            a_chunk = 32 * (NG // OSLOTS)
            mine = [sum(n for _, n in out_halves(i)) if tail else 2 for i in range(slot, NG, OSLOTS)]
            return j * a_chunk + OEV + 16 * sum(mine[:groups])

        @block.sync
        def _(sp):
            def halves(dst, src):
                sp.dma_start(dst[:, 0, :], src[0:P, :]).then_inc(s_par, 16)
                sp.dma_start(dst[0:HR, 1, :], src[P:F, :]).then_inc(s_par, 16)

            sp.wait_ge(s_zero, 1)
            for dst, src in ((lAr, log_A_real), (Aim, A_imag), (Cr, C_re), (Ci, C_im)):
                halves(dst, src)
            for dst, src in ((ldt, log_dt), (dsk, Dskip)):
                col = src.rearrange("(h a) -> h a", a=1)
                sp.dma_start(dst[:, 0:1], col[0:P, :]).then_inc(s_par, 16)
                sp.dma_start(dst[0:HR, 1:2], col[P:F, :]).then_inc(s_par, 16)
            for dst, src in ((WgL, Wg), (WiL, Wi)):
                for h in range(2):
                    sp.dma_start(dst[0:C, C * h:C * h + C], src[:, :, 0, 0]).then_inc(s_wts, 16)
            for h in range(2):
                sp.dma_start(WcL[0:C, 3 * C * h:3 * C * h + 3 * C],
                             Wc.rearrange("o c k a -> o (c k a)")).then_inc(s_wts, 16)
            for i in range(3):
                n = min(P, O2 - i * P)
                sp.dma_start(WoL[0:n, i, :], Wout[i * P:i * P + n, :]).then_inc(s_wts, 16)
                sp.dma_start(boL[0:n, i:i + 1], bout.rearrange("(h a) -> h a", a=1)[i * P:i * P + n, :])\
                  .then_inc(s_wts, 16)
            for dst, src in zip(wraw, (w0, b0, w1, b1)):
                for h in range(2):
                    sp.dma_start(dst[64 * h:64 * h + 64, 0:F], src[0, :, :, 0]).then_inc(s_wts, 16)
            for h in range(2):
                sp.dma_start(bc2[64 * h:64 * h + 64, :], bc.rearrange("(h a) -> h a", a=1)).then_inc(s_wts, 16)
            for row, src in ((bg1, bg), (bi1, bi)):
                sp.dma_start(row[0:1, :], src.rearrange("(a h) -> a h", a=1)).then_inc(s_wts, 16)

            def load_x(b, k, g):
                sp.wait_ge(s_xt, NG * (b * PER_B + k) + g + 1)
                for h in range(2):
                    m = (freqs_of(g) + 1 - h) // 2
                    if m:
                        src = bass.AP(x.tensor, b * (C * F * T) + k * P + (2 * GP * g + h) * T,
                                      [[F * T, C], [2 * T, m], [1, P]])
                        sp.dma_start(xring[64 * h:64 * h + 64, g % XSLOTS, 0:m, :], src)\
                          .then_inc(s_x[g % XSLOTS], 16 * m)

            def load_tail(g):
                sp.wait_ge(s_xt, NG * NCHUNK + g + 1)
                for i in range(freqs_of(g)):
                    src = bass.AP(x.tensor, (2 * GP * g + i) * T + PER_B * P,
                                  [[F * T, C], [C * F * T, B], [1, TAIL]])
                    dst = xring[64 * (i % 2):64 * (i % 2) + 64, g % XSLOTS, i // 2, :]
                    sp.dma_start(dst.rearrange("c (b t) -> c b t", b=B), src).then_inc(s_x[g % XSLOTS], 16)

            sp.wait_ge(s_kpad, 1)
            sp.dma_start(kdram[0:P, :], tsb[:, 0, :, :].rearrange("p j l -> p (j l)")).then_inc(s_kd, 16)
            sp.dma_start(kdram[P:F, :], tsb[0:HR, 1, :, :].rearrange("p j l -> p (j l)")).then_inc(s_kd, 16)
            sp.wait_ge(s_kd, 32)
            for h in range(2):
                n = PAIRS - h
                sp.dma_start(toep[64 * h:64 * h + 64, 0:n, :],
                             bass.AP(kdram.tensor, h * C * C, [[C, C], [2 * C * C, n], [1, C]]))\
                  .then_inc(s_toep, 16)

            with sp.Fori(0, B) as b:
                with sp.Fori(0, PER_B) as k:
                    for g in range(NG):
                        load_x(b, k, g)
            for g in range(NG):
                load_tail(g)
            for s in range(OSLOTS):
                sp.wait_ge(s_st[s], stored(NCHUNK, NG // OSLOTS, s, True))

        @block.gpsimd
        def _(pool):
            done = [0]

            def step(ins):
                done[0] += 1
                ins.then_inc(s_pset, 1)
                pool.wait_ge(s_pset, done[0])

            step(pool.memset(ident[:, :], 0.0))
            step(pool.affine_select(out=ident[:, :], in_=ident[:, :], compare_op=ALU.not_equal, fill=1.0,
                                    base=0, pattern=[[-1, P]], channel_multiplier=1))
            step(pool.tensor_copy(identb[:, :], ident[:, :]))
            step(pool.memset(half[:, :], 0.5))
            pool.wait_ge(s_ready, 1)

            def chunk(j):
                def low(i):
                    pool.wait_ge(s_zhi, NLG * j + i + 1)
                    pool.tensor_tensor(zr[:, i % 2, :, HR:2 * HR], z[:, LG * i:LG * i + LG, H0:F],
                                       zr[:, i % 2, :, 0:HR], ALU.subtract).then_inc(s_zr, 1)

                def add(s):
                    pool.wait_ge(s_glu, NSUB * j + s + 1)
                    dst = x1[:, 0:F, 2 * s:2 * s + 2]
                    pool.tensor_tensor(dst, dst, glu[:, s % 2, :, :].rearrange("p c f -> p f c"),
                                       ALU.add).then_inc(s_add, 1)

                low(0)
                low(1)
                for i in range(NLG):
                    if i + 2 < NLG:
                        low(i + 2)
                    add(2 * i)
                    add(2 * i + 1)
                for at in (0, LN1):
                    pool.wait_ge(s_ln, LN * j + at + 2)
                    pool.tensor_tensor(std[:, :], var_n[:, :], half[:, :], ALU.pow).then_inc(s_std, 1)

            with pool.Fori(0, NCHUNK + 1) as j:
                chunk(j)

        @block.scalar
        def _(act):
            act.wait_ge(s_par, 12 * 16)
            act.activation(dt_, ldt, ACT.Exp).then_inc(s_exp, 1)
            act.activation(eA, lAr, ACT.Exp).then_inc(s_exp, 1)
            act.wait_ge(s_arg, 1)
            act.activation(th, ah, ACT.Tanh).then_inc(s_trig, 1)
            act.activation(sn, ang, ACT.Sin).then_inc(s_trig, 1)
            act.activation(sh, ang, ACT.Sin, scale=0.5).then_inc(s_trig, 1)
            act.wait_ge(s_ready, 1)

            def gelu(j, g):
                nf = freqs_of(g)
                act.wait_ge(s_conv, NG * j + g + 1)
                act.activation(z[:, :, 2 * GP * g:2 * GP * g + nf],
                               ps[:, 2 + g % 2, 0:C * nf].rearrange("p (h l) -> p l h", h=nf),
                               ACT.Gelu).then_inc(s_gelu, 1)

            def chunk(j):
                for g in range(NG):
                    nf = freqs_of(g)
                    if g >= EARLY:
                        gelu(j, g)
                    act.wait_ge(s_xt, NG * j + g + 1 + XSLOTS)
                    act.activation(xf[:, 2 * GP * C * g:2 * GP * C * g + C * nf], ps[:, g % 2, 0:C * nf],
                                   ACT.Copy).then_inc(s_xtev, 1)

                def sigmoid(s):
                    act.wait_ge(s_y, NSUB * j + s + 1)
                    if s >= 2:
                        act.wait_ge(s_glu, NSUB * j + s - 1)
                    bank = 4 + 2 * (s % 2)
                    act.activation(sig[:, s % 2, :, :], ps[:, bank:bank + 2, F:O2], ACT.Sigmoid).then_inc(s_sig, 1)

                def last_parts(i):
                    if i >= 2:
                        act.wait_ge(s_rT, NLG * j + i - 1)
                    src = z[:, LG * i:LG * i + LG, H0:F]
                    if i == 0:
                        act.wait_ge(s_gelu, NG * j + NG)
                    act.activation(zr[:, i % 2, :, 0:HR].bitcast(F32R), src, ACT.Copy)
                    act.activation(zr[:, i % 2, :, 2 * HR:3 * HR], src, ACT.Copy).then_inc(s_zhi, 1)

                for s in range(OSLOTS):
                    act.wait_ge(s_st[s], stored(j, 0, s, False))
                last_parts(0)
                last_parts(1)
                for i in range(NLG + 1):
                    if i < NLG:
                        act.wait_ge(s_zT, NLG * j + i + 1)
                        if i >= 2:
                            act.wait_ge(s_y, NSUB * j + 2 * i - 2)
                        act.activation(zh[:, i % 2, :, :], ps[:, 2 + i % 2, :].rearrange("p (l t) -> p l t", l=LG),
                                       ACT.Copy).then_inc(s_zh, 1)
                        act.wait_ge(s_rT, NLG * j + i + 1)
                        act.activation(zrT[0:KR, i % 2, :, :],
                                       ps[0:KR, i % 2, :].rearrange("p (l t) -> p l t", l=LG),
                                       ACT.Copy).then_inc(s_zrT, 1)
                        if i + 2 < NLG:
                            last_parts(i + 2)
                    if i >= 1:
                        sigmoid(2 * i - 2)
                        sigmoid(2 * i - 1)

                def x1_copy(g):
                    n = pairs_of(g)
                    act.wait_ge(s_x1T, NG * j + g + 1)
                    if g >= 2:
                        act.wait_ge(s_gw, NG * j + g - 1)
                    act.activation(x1c[:, g % 2, 0:n, :], ps[:, g % 2, 0:P * n].rearrange("p (n t) -> p n t", n=n),
                                   ACT.Copy).then_inc(s_x1c, 1)

                def gate_of(q):
                    w = C * freqs_of(q)
                    act.wait_ge(s_gw, NG * j + q + 1)
                    if q >= 2:
                        act.wait_ge(s_v, NG * j + q - 1)
                    act.activation(gate[:, q % 2, 0:w], ps[:, 4 + q % 2, 0:w], ACT.Sigmoid,
                                   scale=rstd[:, 0:1]).then_inc(s_gate, 1)

                x1_copy(0)
                x1_copy(1)
                for g in range(2, NG + 2):
                    if g < NG:
                        x1_copy(g)
                    gate_of(g - 2)

            def store(b, k, g):
                j = NCHUNK if b is None else b * PER_B + k
                act.wait_ge(s_oev, NG * j + g + 1 + OEV)
                for h, (q, n) in enumerate(out_halves(g)):
                    src = oring[64 * h:64 * h + 64, g % OSLOTS, q - GP * g:q - GP * g + n, :]
                    f0 = 2 * q - 1 + h
                    if b is not None:
                        dst = bass.AP(out.tensor, b * (C * F * T) + k * P + f0 * T, [[F * T, C], [2 * T, n], [1, P]])
                        act.dma_start(dst, src).then_inc(s_st[g % OSLOTS], 16)
                        continue
                    for i in range(n):
                        dst = bass.AP(out.tensor, (f0 + 2 * i) * T + PER_B * P,
                                      [[F * T, C], [C * F * T, B], [1, TAIL]])
                        act.dma_start(dst, src[:, i, :].rearrange("c (b t) -> c b t", b=B))\
                           .then_inc(s_st[g % OSLOTS], 16)

            def last_phase(b, k):
                j = NCHUNK if b is None else b * PER_B + k
                early = EARLY if b is not None else 0

                def norm(g):
                    if g == 0:
                        act.wait_ge(s_ln, LN * j + LN)
                    v = xf[:, 2 * GP * C * g:2 * GP * C * g + C * freqs_of(g)]
                    act.activation(v, v, ACT.Identity, scale=rstd[:, 0:1], bias=nmr[:, 0:1]).then_inc(s_n, 1)

                def high(g):
                    n = pairs_of(g)
                    act.wait_ge(s_vw, NG * j + g + 1)
                    if g >= VSLOTS:
                        act.wait_ge(s_o, NG * j + g - VSLOTS + 2)
                    act.activation(vh[:, g % VSLOTS, 0:n, :], vw[:, g % 2, 0:n, :], ACT.Copy).then_inc(s_vh, 1)

                for g in range(max(early - 2, 0)):
                    gelu(j + 1, g)
                for g in range(2):
                    norm(g)
                    if early:
                        gelu(j + 1, early - 2 + g)
                for g in range(NG):
                    if g + 2 < NG:
                        norm(g + 2)
                    high(g)
                    if g >= SLAG:
                        store(b, k, g - SLAG)
                for g in range(NG - SLAG, NG):
                    store(b, k, g)

            for g in range(EARLY):
                gelu(0, g)
            with act.Fori(0, B) as b:
                with act.Fori(0, PER_B) as k:
                    chunk(b * PER_B + k)
                    last_phase(b, k)
            chunk(NCHUNK)
            last_phase(None, None)

        @block.tensor
        def _(pe):
            pe.wait_ge(s_pset, 4)
            pe.wait_ge(s_rows, 1)
            pe.transpose(ps[:, 0, 0:C], WgL[0:C, :], ident[0:C, 0:C])
            pe.transpose(ps[:, 0, C:2 * C], WiL[0:C, :], ident[0:C, 0:C])
            for k in range(3):
                pe.transpose(ps[:, 1, C * k:C * k + C], WcL[0:C, :].rearrange("o (c k) -> o k c", k=3)[:, k, :],
                             ident[0:C, 0:C])
            for i in range(3):
                n = min(P, O2 - i * P)
                pe.transpose(ps[:, 2, i * P:i * P + n], WoL[0:n, i, 0:H0], ident[0:n, 0:n])
                pe.transpose(ps[0:KR, 3, i * P:i * P + n], WoR[0:n, i, :], ident[0:n, 0:n])
            for i in range(3):
                pe.matmul(ps[:, 4, 2 * i:2 * i + 2], pmask[0:1, i, :], one1[0:1, :], start=True, stop=True)
            pe.matmul(ps[:, 5, :], mI[0:1, :], birow[0:1, :, :].rearrange("p a b -> p (a b)"), start=True,
                      stop=True).then_inc(s_wT, 1)
            for s in range(-(-NG // 4)):
                groups = range(4 * s, min(4 * s + 4, NG))
                if s >= 2:
                    pe.wait_ge(s_rgev, s - 1)
                for g in groups:
                    n = pairs_of(g)
                    o = ps[:, 6 + s % 2, 0:P * n]
                    at = WIN - 32 * (g % 4)
                    pe.wait_ge(s_gb, g + 1)
                    pe.matmul(o, mA[:, at:at + P], G[:, GP * g:GP * g + n, :].rearrange("p a b -> p (a b)"),
                              start=(g == groups[0]), stop=False, skip_group_check=True)
                    pe.matmul(o, mB[0:1, at:at + P], bgrow[0:1, 0:2 * n, :].rearrange("p a b -> p (a b)"),
                              start=False, stop=False, skip_group_check=True)
                    pe.matmul(o, mB[:, at:at + P], Gb[:, 0:n, :].rearrange("p a b -> p (a b)"),
                              start=False, stop=(g == groups[-1]), skip_group_check=True).then_inc(s_gbu, 1)
            pe.matmul(ps[:, 0, 0:PAIRS], Wself[:, :], b1c, start=True, stop=False, skip_group_check=True)
            pe.matmul(ps[:, 0, 1:PAIRS], Wprev[:, :], b1c[:, 0:PAIRS - 1], start=False, stop=True,
                      skip_group_check=True).then_inc(s_ob, 1)
            pe.wait_ge(s_ready, 1)

            def s4d(j, g):
                pe.wait_ge(s_t, 2 * NG * j + 2 * g + 2)
                pe.wait_ge(s_x[g % XSLOTS], x_landed(j, g))
                if g >= 2:
                    pe.wait_ge(s_gelu, NG * j + g - 1)
                for i in range(pairs_of(g)):
                    ins = pe.matmul(ps[:, 2 + g % 2, P * i:P * i + P], xring[:, g % XSLOTS, i, :],
                                    tring[:, g % 3, i, :], start=True, stop=True)
                ins.then_inc(s_conv, 1)

            def chunk(j, tail):
                for g in range(NG):
                    if g >= EARLY:
                        s4d(j, g)
                    if g >= 2:
                        pe.wait_ge(s_xtev, NG * j + g - 1)
                    for i in range(pairs_of(g)):
                        ins = pe.transpose(ps[:, g % 2, P * i:P * i + P], xring[:, g % XSLOTS, i, :], ident[:, :])
                    ins.then_inc(s_xt, 1)
                pe.wait_ge(s_gelu, NG * j + NG)
                for i in range(NLG + 1):
                    if i < NLG:
                        if i >= 2:
                            pe.wait_ge(s_zl, NLG * j + i - 1)
                        for c in range(LG):
                            ins = pe.transpose(ps[:, 2 + i % 2, P * c:P * c + P], z[:, LG * i + c, 0:H0], ident[:, :])
                        ins.then_inc(s_zT, 1)
                        pe.wait_ge(s_zr, NLG * j + i + 1)
                        if i == 0:
                            pe.wait_ge(s_xtev, NG * j + NG)
                            pe.wait_ge(s_one, j + 1)
                        if i >= 2:
                            pe.wait_ge(s_zrT, NLG * j + i - 1)
                        for c in range(LG):
                            ins = pe.transpose(ps[0:KR, i % 2, P * c:P * c + P], zr[:, i % 2, c, :],
                                               ident[:, :])
                        ins.then_inc(s_rT, 1)
                    if i >= 1:
                        k = (i - 1) % 2
                        pe.wait_ge(s_zrT, NLG * j + i)
                        pe.wait_ge(s_zl, NLG * j + i)
                        for s in (2 * i - 2, 2 * i - 1):
                            if s == 0:
                                pe.wait_ge(s_oev, NG * j + OEV)
                            if s >= 2:
                                pe.wait_ge(s_glu, NSUB * j + s - 1)
                            for c in range(2):
                                o = ps[:, 4 + 2 * (s % 2) + c, 0:O2]
                                l = 2 * (s % 2) + c
                                pe.matmul(o, zh[:, k, l, :], Wh[:, :], start=True, stop=False)
                                pe.matmul(o, zh[:, k, l, :], Wl[:, :], start=False, stop=False)
                                pe.matmul(o, zl[:, k, l, :], Wh[:, :], start=False, stop=False)
                                ins = pe.matmul(o, zrT[0:KR, k, l, :], Wr[:, :], start=False, stop=True)
                            ins.then_inc(s_y, 1)
                pe.wait_ge(s_add, NSUB * j + NSUB)
                def x1_channels(g):
                    if g >= 2:
                        pe.wait_ge(s_x1c, NG * j + g - 1)
                    for i in range(pairs_of(g)):
                        f = 2 * (GP * g + i)
                        ins = pe.transpose(ps[:, g % 2, P * i:P * i + P], xf[:, C * f:C * f + P], ident[:, :])
                    ins.then_inc(s_x1T, 1)

                def gate_products(k):
                    pe.wait_ge(s_x1c, NG * j + k + 1)
                    if k == 0:
                        pe.wait_ge(s_glu, NSUB * j + NSUB)
                    if k >= 2:
                        pe.wait_ge(s_v, NG * j + k - 1)
                    for i in range(pairs_of(k)):
                        pe.matmul(ps[:, 4 + k % 2, P * i:P * i + P], x1c[:, k % 2, i, :], G[:, GP * k + i, :],
                                  start=(i == 0), stop=False, skip_group_check=True)
                        pe.matmul(ps[:, 6 + k % 2, P * i:P * i + P], x1c[:, k % 2, i, :], Wib[:, :],
                                  start=(i == 0), stop=False, skip_group_check=True)

                def rank_one(k):
                    w = P * pairs_of(k)
                    pe.matmul(ps[:, 4 + k % 2, 0:w], Lt[:, k % 4, :], Rg[:, GP * P * (k // 4):GP * P * (k // 4) + w],
                              start=False, stop=True, skip_group_check=True)
                    pe.matmul(ps[:, 6 + k % 2, 0:w], Lt[:, 0, :], Rw[:, 0:w],
                              start=False, stop=True, skip_group_check=True).then_inc(s_gw, 1)

                x1_channels(0)
                x1_channels(1)
                gate_products(0)
                gate_products(1)
                pe.wait_ge(s_ln, LN * j + LN1)
                for q in range(4):
                    at = WIN - 32 * q
                    ins = pe.transpose(ps[:, 2, 0:256].bitcast(BF16)[:, P * q:P * q + P],
                                       Lsrc[:, at:at + P], identb[:, :])
                ins.then_inc(s_LT, 1)
                pe.wait_ge(s_Lt, j + 1)
                rank_one(0)
                x1_channels(2)
                rank_one(1)
                for k in range(2, NG):
                    if k + 1 < NG:
                        x1_channels(k + 1)
                    gate_products(k)
                    rank_one(k)
                def v_channels(g):
                    pe.wait_ge(s_n, NG * j + g + 1)
                    if g >= 2:
                        pe.wait_ge(s_vw, NG * j + g - 1)
                    for i in range(pairs_of(g)):
                        f = 2 * (GP * g + i)
                        ins = pe.transpose(ps[:, g % 2, P * i:P * i + P], xf[:, C * f:C * f + P], ident[:, :])
                    ins.then_inc(s_vT, 1)

                def conv(k):
                    n = pairs_of(k)
                    pe.wait_ge(s_vl, NG * j + k + 1)
                    if k >= 2:
                        pe.wait_ge(s_oev, NG * j + k - 1 + OEV)
                    o = ps[:, 4 + k % 2, :]
                    now, last = k % VSLOTS, (k - 1) % VSLOTS
                    work = []
                    for hl, (v, ws, wp) in enumerate(((vh, Wself_h, Wprev_h), (vh, Wself_l, Wprev_l),
                                                      (vl, Wself_h, Wprev_h))):
                        work.append((o[:, 0:P * n], ws, v[:, now, 0:n, :]))
                        if k > 0:
                            work.append((o[:, 0:P], wp, v[:, last, GP - 1:GP, :]))
                        if n > 1:
                            work.append((o[:, P:P * n], wp, v[:, now, 0:n - 1, :]))
                    for m, (cols, w, v) in enumerate(work):
                        ins = pe.matmul(cols, w[:, :], v.rearrange("p n t -> p (n t)"), start=(m == 0),
                                        stop=(m == len(work) - 1), skip_group_check=True)
                    ins.then_inc(s_o, 1)

                early = EARLY if not tail else 0
                for g in range(max(early - 1, 0)):
                    s4d(j + 1, g)
                v_channels(0)
                if early:
                    s4d(j + 1, early - 1)
                v_channels(1)
                for g in range(2, NG + 2):
                    if g < NG:
                        v_channels(g)
                    conv(g - 2)

            for g in range(EARLY):
                s4d(0, g)
            with pe.Fori(0, NCHUNK) as j:
                chunk(j, False)
            chunk(NCHUNK, True)

        @block.vector
        def _(dve):
            done = [0]

            def step(ins):
                done[0] += 1
                ins.then_inc(s_set, 1)
                dve.wait_ge(s_set, done[0])

            def tt(o, a, b, op):
                step(dve.tensor_tensor(o, a, b, op))

            def ts(o, a, s1, s2, op0, op1=ALU.bypass):
                step(dve.tensor_scalar(o, a, s1, s2, op0, op1) if s2 is not None
                     else dve.tensor_scalar(o, a, s1, None, op0))

            def stt(o, a, s, b, op0, op1):
                step(dve.scalar_tensor_tensor(out=o, in0=a, scalar=s, in1=b, op0=op0, op1=op1))

            add, sub, mul = ALU.add, ALU.subtract, ALU.mult
            dve.memset(xf, 0.0).then_inc(s_zero, 1)
            step(dve.memset(zf, 0.0))
            step(dve.memset(tring[:, :, :, :], 0.0))
            step(dve.memset(G[:, :, :], 0.0))
            step(dve.memset(toep[64:P, PAIRS - 1, :], 0.0))
            for m in (Wib, Wself, Wprev, Lsrc, w1c):
                step(dve.memset(m[:, :], 0.0))
            step(dve.memset(Lsrc[:, WIN + K_ONE:WIN + K_ONE + 3], 1.0))
            step(dve.memset(mA[:, WIN + K_MEAN:WIN + K_MEAN + NSP], -1.0))
            step(dve.memset(mB[:, WIN + K_STD:WIN + K_STD + NSP], 1.0))
            step(dve.memset(mI[:, K_ONE:K_ONE + 3], 1.0))
            step(dve.memset(one1, 1.0))
            dve.memset(ms[:, :], 0.0).then_inc(s_xt, XSLOTS)
            dve.memset(rstd[:, :], 0.0).then_inc(s_oev, OEV)
            for s in s_st:
                dve.memset(res[:, :], 0.0).then_inc(s, OEV)
                dve.wait_ge(s, OEV)
            dve.wait_ge(s_oev, OEV)
            dve.wait_ge(s_zero, 1)
            for k, part in [(K_MEAN + i, r) for i, (_, r) in enumerate(SPLITS)]\
                    + [(K_STD + i, r) for i, (_, r) in enumerate(SPLITS)] + [(K_ONE + i, i) for i in range(3)]:
                step(dve.memset(pmask[0:1, part, :].rearrange("p (q k) -> p q k", q=4)[:, :, k], 1.0))

            dve.wait_ge(s_exp, 2)
            dtb = dt_.unsqueeze(2).to_broadcast([P, 2, NS])
            tt(t1, eA, dtb, mul)
            ts(ah, t1, -0.5, None, mul)
            tt(bb, Aim, dtb, mul)
            magic = 12582912.0
            ts(kf, bb, 1.0 / TWO_PI, magic, mul, add)
            ts(t1, kf, magic, None, sub)
            rest = TWO_PI
            c1 = 6.28125
            c2 = 0.0019350051879882812
            c3 = rest - c1 - c2
            stt(t2, t1, -c1, bb, mul, add)
            stt(t3, t1, -c2, t2, mul, add)
            stt(t2, t1, -c3, t3, mul, add)
            dve.tensor_scalar(ang, t2, 3.1415925, -3.1415925, ALU.min, ALU.max).then_inc(s_arg, 1)
            dve.wait_ge(s_trig, 3)
            tt(t1, sh, sh, mul)
            ts(t1, t1, -2.0, None, mul)
            ts(cs, t1, 1.0, None, add)
            ts(t2, th, -1.0, 1.0, mul, add)
            step(dve.reciprocal(t3, t2))
            tt(t2, th, t3, mul)
            ts(em, t2, 2.0, None, mul)
            ts(ea, em, 1.0, None, add)
            tt(wr, ea, cs, mul)
            tt(wi, ea, sn, mul)
            tt(t2, em, cs, mul)
            tt(em, t2, t1, add)
            ts(eA, eA, -1.0, None, mul)
            tt(t1, Cr, em, mul)
            tt(t2, Ci, wi, mul)
            tt(t3, t1, t2, sub)
            tt(t1, Cr, wi, mul)
            tt(t2, Ci, em, mul)
            tt(cs, t1, t2, add)
            tt(t1, eA, eA, mul)
            tt(t2, Aim, Aim, mul)
            tt(t1, t1, t2, add)
            step(dve.reciprocal(t2, t1))
            ts(t2, t2, 2.0, None, mul)
            tt(t1, t3, eA, mul)
            tt(ea, cs, Aim, mul)
            tt(t1, t1, ea, add)
            tt(Qr[:, :, 0, :], t1, t2, mul)
            tt(t1, cs, eA, mul)
            tt(ea, t3, Aim, mul)
            tt(t1, t1, ea, sub)
            tt(Qi[:, :, 0, :], t1, t2, mul)
            s = 1
            while s < C:
                wrb = wr.unsqueeze(2).to_broadcast([P, 2, s, NS])
                wib = wi.unsqueeze(2).to_broadcast([P, 2, s, NS])
                lo_r, lo_i, hi_r, hi_i = Qr[:, :, 0:s], Qi[:, :, 0:s], Qr[:, :, s:2 * s], Qi[:, :, s:2 * s]
                tt(Ta[:, :, 0:s], lo_r, wrb, mul)
                tt(Tb[:, :, 0:s], lo_i, wib, mul)
                tt(hi_r, Ta[:, :, 0:s], Tb[:, :, 0:s], sub)
                if 2 * s < C:
                    tt(Ta[:, :, 0:s], lo_r, wib, mul)
                    tt(Tb[:, :, 0:s], lo_i, wrb, mul)
                    tt(hi_i, Ta[:, :, 0:s], Tb[:, :, 0:s], add)
                    tt(t1, wr, wr, mul)
                    tt(t2, wi, wi, mul)
                    tt(t3, wr, wi, mul)
                    tt(wr, t1, t2, sub)
                    ts(wi, t3, 2.0, None, mul)
                s *= 2
            step(dve.tensor_reduce(kpad[:, :, C - 1:2 * C - 1], Qr, AX.X, add))
            k0 = kpad[:, :, C - 1]
            tt(k0, k0, dsk, add)
            for i in range(C):
                ins = dve.tensor_copy(tsb[:, :, i, :], kpad[:, :, C - 1 - i:2 * C - 1 - i])
            ins.then_inc(s_kpad, 1)

            dve.wait_ge(s_wts, 16 * 24)
            last = WoL[:, :, H0:F]
            step(dve.tensor_copy(WoR[:, :, 0:HR].bitcast(F32R), last))
            step(dve.tensor_copy(WoR[:, :, HR:2 * HR].bitcast(F32R), last))
            tt(WoR[:, :, 2 * HR:3 * HR], last, WoR[:, :, 0:HR], sub)
            step(dve.tensor_copy(WoR[:, :, 3 * HR].bitcast(F32R), boL))
            tt(WoR[:, :, 3 * HR + 1], boL, WoR[:, :, 3 * HR], sub)
            for row, src in ((bgrow, bg1), (birow, bi1)):
                step(dve.tensor_copy(row[0:1, :, :], src[0:1, :].unsqueeze(1).to_broadcast([1, 2 * GP, C])))
            for dst, src in zip((w0c, b0c, w1c[:, :], b1c), wraw):
                step(dve.tensor_copy(dst[0:C, :], src[0:C, 0:F:2]))
                step(dve.tensor_copy(dst[C:P, 0:PAIRS - 1], src[C:P, 1:F:2]))
            dve.memset(mv[:, :], 0.0).then_inc(s_rows, 1)
            dve.wait_ge(s_wT, 1)
            step(dve.tensor_copy(WgT, ps[:, 0, 0:C]))
            for h in range(2):
                r = slice(C * h, C * h + C)
                step(dve.tensor_copy(Wib[r, r], ps[r, 0, C:2 * C]))
                step(dve.tensor_copy(Wself[r, C:P], ps[r, 1, C * (1 + h):C * (2 + h)]))
                step(dve.tensor_copy(Wprev[r, 0:C], ps[r, 1, C * h:C * h + C]))
            step(dve.tensor_copy(Wself[0:C, 0:C], ps[0:C, 1, 2 * C:3 * C]))
            step(dve.tensor_copy(Wprev[C:P, C:P], ps[C:P, 1, 0:C]))
            for w, w_h, w_l in ((Wself, Wself_h, Wself_l), (Wprev, Wprev_h, Wprev_l)):
                step(dve.tensor_copy(w_h[:, :], w[:, :]))
                tt(w_l[:, :], w[:, :], w_h[:, :].bitcast(F32), sub)
            step(dve.tensor_copy(Wh[:, :], ps[:, 2, 0:O2]))
            tt(Wl[:, :], ps[:, 2, 0:O2], Wh[:, :].bitcast(F32), sub)
            step(dve.tensor_copy(Wr[:, :], ps[0:KR, 3, 0:O2]))
            step(dve.tensor_copy(pm, ps[:, 4, 0:6:2]))
            for h in range(2):
                r = slice(C * h, C * h + C)
                tt(G[r, :, r], WgT[r, :].unsqueeze(1).to_broadcast([C, PAIRS, C]),
                   w0c[r, :].unsqueeze(2).to_broadcast([C, PAIRS, C]), mul)

            def split(bank, w, dst):
                src = ps[:, bank, 0:w]
                step(dve.tensor_copy(hb[0][:, 0:w], src))
                tt(sa[:, 0:w], src, hb[0][:, 0:w], sub)
                step(dve.tensor_copy(hb[1][:, 0:w], sa[:, 0:w]))
                tt(sb_[:, 0:w], sa[:, 0:w], hb[1][:, 0:w], sub)
                step(dve.tensor_copy(hb[2][:, 0:w], sb_[:, 0:w]))
                ts(sa[:, 0:w], hb[0][:, 0:w], pm[:, 0:1], None, mul)
                stt(sc[:, 0:w], hb[1][:, 0:w], pm[:, 1:2], sa[:, 0:w], mul, add)
                return dve.scalar_tensor_tensor(out=dst, in0=hb[2][:, 0:w], scalar=pm[:, 2:3], in1=sc[:, 0:w],
                                                op0=mul, op1=add)

            step(split(5, P * GP, Rw[:, :]))
            for g in range(NG):
                n = pairs_of(g)
                if g >= 1:
                    dve.wait_ge(s_gbu, g)
                for h in range(2):
                    r = slice(C * h, C * h + C)
                    ins = dve.tensor_tensor(Gb[r, 0:n, r], WgT[r, :].unsqueeze(1).to_broadcast([C, n, C]),
                                            b0c[r, GP * g:GP * g + n].unsqueeze(2).to_broadcast([C, n, C]), mul)
                    if h == 0:
                        step(ins)
                ins.then_inc(s_gb, 1)
                if g % 4 == 3 or g == NG - 1:
                    w = P * (GP if g % 4 == 3 else n)
                    dve.wait_ge(s_gbu, g + 1)
                    split(6 + (g // 4) % 2, w, Rg[:, GP * P * (g // 4):GP * P * (g // 4) + w]).then_inc(s_rgev, 1)
                    dve.wait_ge(s_rgev, g // 4 + 1)
            dve.wait_ge(s_ob, 1)
            ts(obias[:, :], ps[:, 0, 0:PAIRS], bc2, None, add)
            dve.memset(xf[:, C * F:], 0.0).then_inc(s_ready, 1)
            dve.wait_ge(s_ready, 1)
            dve.wait_ge(s_toep, 32)

            def toeplitz(j, g):
                n = pairs_of(g)
                if g >= 3:
                    dve.wait_ge(s_conv, NG * j + g - 2)
                for h in range(2):
                    dve.tensor_copy(tring[64 * h:64 * h + 64, g % 3, 0:n, 64 * h:64 * h + 64],
                                    toep[64 * h:64 * h + 64, GP * g:GP * g + n, :]).then_inc(s_t, 1)

            def chunk(j, tail):
                for g in range(EARLY, NG):
                    toeplitz(j, g)
                for s in range(OSLOTS):
                    dve.wait_ge(s_st[s], stored(j, 0, s, False))
                dve.memset(zr[:, :, :, 3 * HR:KR].rearrange("p s c k -> p (s c) k"), 1.0).then_inc(s_one, 1)
                def bn1(s):
                    dve.wait_ge(s_add, NSUB * j + s + 1)
                    dve.bn_stats(stats[:, s, :], x1[:, 0:F, 2 * s:2 * s + 2]).then_inc(s_bn1, 1)

                for i in range(NLG + 1):
                    if i < NLG:
                        dve.wait_ge(s_zh, NLG * j + i + 1)
                        if i >= 2:
                            dve.wait_ge(s_y, NSUB * j + 2 * i - 2)
                        dve.tensor_tensor(zl[:, i % 2, :, :], ps[:, 2 + i % 2, :].rearrange("p (l t) -> p l t", l=LG),
                                          zh[:, i % 2, :, :].bitcast(F32), sub).then_inc(s_zl, 1)
                    if i >= 1:
                        for s in (2 * i - 2, 2 * i - 1):
                            dve.wait_ge(s_sig, NSUB * j + s + 1)
                            if s >= 2:
                                dve.wait_ge(s_add, NSUB * j + s - 1)
                            bank = 4 + 2 * (s % 2)
                            dve.tensor_tensor(glu[:, s % 2, :, :], ps[:, bank:bank + 2, 0:F], sig[:, s % 2, :, :],
                                              mul).then_inc(s_glu, 1)
                            if s >= 2:
                                bn1(s - 2)
                bn1(NSUB - 2)
                bn1(NSUB - 1)

                at = [LN * j]

                def ln_step(ins):
                    at[0] = at[0] + 1
                    ins.then_inc(s_ln, 1)
                    dve.wait_ge(s_ln, at[0])

                def std_of(nstats, roots, meanwhile=None):
                    ln_step(dve.bn_aggr(mv[:, :], stats[:, 0:nstats, :]))
                    ln_step(dve.tensor_scalar(var_n[:, :], mv[:, 1:2], float(NTOT) / (NTOT - 1), None, mul))
                    if meanwhile:
                        meanwhile()
                    dve.wait_ge(s_std, roots)
                    ln_step(dve.tensor_scalar(ms[:, 1:2], std[:, :], 1e-8, None, add))
                    ln_step(dve.reciprocal(rstd[:, :], ms[:, 1:2]))

                dve.wait_ge(s_ready, 1)
                dve.wait_ge(s_bn1, NSUB * j + NSUB)
                std_of(NSUB, 2 * j + 1)
                ln_step(dve.tensor_copy(ms[:, 0:1], mv[:, 0:1]))
                fac = Lsrc[:, WIN:WIN + 2 * NSP].rearrange("p (m k) -> p m k", m=2)
                rest = ms[:, :]
                for part in range(3):
                    ks = [k for k, (lp, _) in enumerate(SPLITS) if lp == part]
                    ln_step(dve.tensor_copy(fac[:, :, ks[0]:ks[-1] + 1],
                                            rest.unsqueeze(2).to_broadcast([P, 2, len(ks)])))
                    if part < 2:
                        ln_step(dve.tensor_tensor(res[:, :], rest, fac[:, :, ks[0]], sub))
                        rest = res[:, :]
                dve.wait_ge(s_LT, j + 1)
                dve.tensor_copy(Lt[:, :, :].rearrange("p q t -> p (q t)"), ps[:, 2, 0:256].bitcast(BF16))\
                   .then_inc(s_Lt, 1)

                def bn2(g):
                    dve.wait_ge(s_v, NG * j + g + 1)
                    v = xf[:, 2 * GP * C * g:2 * GP * C * g + C * freqs_of(g)]
                    dve.bn_stats(stats[:, g, :], v).then_inc(s_bn2, 1)

                early = EARLY if not tail else 0
                for g in range(NG):
                    if g < min(early, 3):
                        toeplitz(j + 1, g)
                    w = C * freqs_of(g)
                    dve.wait_ge(s_gate, NG * j + g + 1)
                    dve.tensor_tensor(xf[:, 2 * GP * C * g:2 * GP * C * g + w], ps[:, 6 + g % 2, 0:w],
                                      gate[:, g % 2, 0:w], mul).then_inc(s_v, 1)
                    if g >= 1:
                        bn2(g - 1)
                bn2(NG - 1)
                dve.wait_ge(s_ready, 1)
                dve.wait_ge(s_bn2, NG * j + NG)
                std_of(NG, 2 * j + 2, (lambda: toeplitz(j + 1, 3)) if early else None)
                ln_step(dve.tensor_scalar(nmr[:, :], mv[:, 0:1], rstd[:, 0:1], -1.0, mul, mul))

                for g in range(4, early):
                    toeplitz(j + 1, g)

                for g in range(NG + 3):
                    if g < NG:
                        n = pairs_of(g)
                        dve.wait_ge(s_vT, NG * j + g + 1)
                        if g >= 2:
                            dve.wait_ge(s_vl, NG * j + g - 1)
                        dve.tensor_tensor(vw[:, g % 2, 0:n, :], ps[:, g % 2, 0:P * n].rearrange("p (n t) -> p n t", n=n),
                                          w1c[:, GP * g:GP * g + n].unsqueeze(2).to_broadcast([P, n, P]),
                                          mul).then_inc(s_vw, 1)
                    if 1 <= g <= NG:
                        q = g - 1
                        n = pairs_of(q)
                        dve.wait_ge(s_vh, NG * j + q + 1)
                        dve.tensor_tensor(vl[:, q % VSLOTS, 0:n, :], vw[:, q % 2, 0:n, :],
                                          vh[:, q % VSLOTS, 0:n, :].bitcast(F32), sub).then_inc(s_vl, 1)
                    if g >= 3:
                        q = g - 3
                        n = pairs_of(q)
                        dve.wait_ge(s_o, NG * j + q + 1)
                        dve.wait_ge(s_st[q % OSLOTS], stored(j, q // OSLOTS, q % OSLOTS, tail))
                        dve.tensor_tensor(oring[:, q % OSLOTS, 0:n, :],
                                          ps[:, 4 + q % 2, 0:P * n].rearrange("p (n t) -> p n t", n=n),
                                          obias[:, GP * q:GP * q + n].unsqueeze(2).to_broadcast([P, n, P]),
                                          add).then_inc(s_oev, 1)

            for g in range(EARLY):
                toeplitz(0, g)
            with dve.Fori(0, NCHUNK) as j:
                chunk(j, False)
            chunk(NCHUNK, True)


_NAMES = ["log_dt", "log_A_real", "A_imag", "C_re", "C_im", "Dskip", "Wout", "bout", "w0", "b0", "w1", "b1",
          "Wg", "bg", "Wi", "bi", "Wc", "bc"]


def kernel(**inputs):
    import numpy as _np
    import concourse.bacc as _bacc
    from concourse import mybir as _mybir
    from concourse.bass_utils import run_bass_kernel_spmd as _run

    nc = _bacc.Bacc("TRN2", target_bir_lowering=False, num_devices=1)
    arrays, args = {}, []
    for name in ["x"] + ["L0_conv_" + n for n in _NAMES]:
        a = _np.ascontiguousarray(inputs[name])
        arrays[f"in_{name}_dram"] = a
        args.append(nc.dram_tensor(f"in_{name}_dram", a.shape, _mybir.dt.from_np(a.dtype),
                                   kind="ExternalInput").ap())
    out = nc.dram_tensor("out_dram", (B, C, F, T), F32, kind="ExternalOutput").ap()
    conv_seq_program(nc, *args, out)
    r = _run(nc, [arrays], core_ids=[0])
    return r.results[0]["out_dram"]
```

```python
from contextlib import ExitStack

import concourse.bass as bass
from concourse import mybir

F32 = mybir.dt.float32
F32R = mybir.dt.float32r
BF16 = mybir.dt.bfloat16
ACT = mybir.ActivationFunctionType
ALU = mybir.AluOpType
AX = mybir.AxisListType

P = 128
B, C, F, T = 8, 64, 161, 400
NS = 32
PAIRS = (F + 1) // 2
GP = 4
NG = -(-PAIRS // GP)
PER_B = T // P
TAIL = T - PER_B * P
NCHUNK = B * PER_B
XSLOTS = 7
XUNITS = [(0, 2), (2, 2), (4, 3)]
GSLOTS = 3
GATE_AT = (6, 9, 12)
OSLOTS = 3
H0 = 128
HR = F - H0
KR = 3 * HR + 2
LG = 4
NLG = C // LG
NSUB = C // 2
O2 = 2 * F
NTOT = C * F
SPLITS = [(0, 0), (0, 1), (0, 2), (1, 0), (1, 1), (2, 0)]
NSP = len(SPLITS)
K_MEAN, K_STD, K_ONE = 0, NSP, 2 * NSP
WIN = P - 32
NSUM = -(-NG // 4)
SUM_BANKS = (6, 7, 1, 2, 3, 4)
LN1, LN2 = 10, 5
LN = LN1 + LN2
EARLY = 7
VSLOTS = 4
SCATTER = (9, 17, NG)
SLAG = 3
LEAD = 2
TWO_PI = 6.283185307179586
assert TAIL * B == P and NG % XSLOTS == 0 and NG % OSLOTS == 0


def pairs_of(g):
    return min(GP, PAIRS - g * GP)


def freqs_of(g):
    return min(2 * GP, F - g * 2 * GP)


def conv_seq_program(nc, x, log_dt, log_A_real, A_imag, C_re, C_im, Dskip, Wout, bout, w0, b0, w1, b1,
                     Wg, bg, Wi, bi, Wc, bc, out):
    ctx = ExitStack()
    with ctx:
        def sb(name, shape, dt=F32):
            return ctx.enter_context(nc.sbuf_tensor(name, shape, dt))

        def sem(name):
            return ctx.enter_context(nc.semaphore(name))

        xring = sb("xring", [P, XSLOTS, GP, P])
        toep = sb("toep", [P, PAIRS, C])
        tring = sb("tring", [P, 3, GP, P])
        z = sb("z", [P, C, F])
        x1 = sb("x1", [P, 2 * PAIRS, C])
        parts = sb("parts", [P, 8, GP * P], F32R)

        def groups_in(at, n):
            return parts[:, at:at + n, :].rearrange("p s (i t) -> p s i t", i=GP)

        zh, zl = groups_in(0, 2), groups_in(2, 2)
        zrT = groups_in(4, 2)
        x1h, x1l = groups_in(0, 2), groups_in(2, 2)
        vh, vl = groups_in(0, VSLOTS), groups_in(VSLOTS, VSLOTS)
        OEND = OSLOTS * GP * P
        turn = sb("turn", [P, OEND + 12 * F // 2 + 2 * LG * KR])

        def piece(at, pattern, **sizes):
            n = 1
            for v in sizes.values():
                n *= v
            return turn[:, at:at + n].rearrange(pattern, **sizes)

        zr = piece(OEND + 4 * F, "p (s c k) -> p s c k", s=2, c=LG, k=KR)
        sig = piece(OEND, "p (s c f) -> p s c f", s=2, c=2, f=F)
        glu = [piece(at, "p (c f) -> p c f", c=2, f=F)
               for at in (OEND + 2 * LG * KR + 4 * F, 0)]
        gate = piece(2 * GP * P, "p (s w) -> p s w", s=2, w=GP * P)
        oring = piece(0, "p (s n t) -> p s n t", s=OSLOTS, n=GP, t=P)
        vw = piece(OEND, "p (s n t) -> p s n t", s=2, n=GP, t=P)
        stats = sb("stats", [P, NSUB, 6])
        mv = sb("mv", [P, 2])
        ms = sb("ms", [P, 2])
        res = sb("res", [P, 2])
        rstd = sb("rstd", [P, 1])
        nmr = sb("nmr", [P, 1])
        var_n = sb("var_n", [P, 1])
        std = sb("std", [P, 1])
        half = sb("half", [P, 1])
        spare = sb("spare", [P, 1])
        Lsrc = sb("Lsrc", [P, 224], BF16)
        Lt = sb("Lt", [P, 4, P], BF16)
        G = sb("G", [P, PAIRS, C])
        gates = sb("gates", [P, 2 * GSLOTS * GP + 2, P], F32R)
        GH, GL, WIH, WIL = 0, GSLOTS * GP, 2 * GSLOTS * GP, 2 * GSLOTS * GP + 1
        Wh = sb("Wh", [P, O2], F32R)
        Wl = sb("Wl", [P, O2], F32R)
        Wr = sb("Wr", [KR, O2], F32R)
        Wself_h, Wself_l = sb("Wself_h", [P, P], F32R), sb("Wself_l", [P, P], F32R)
        Wprev_h, Wprev_l = sb("Wprev_h", [P, P], F32R), sb("Wprev_l", [P, P], F32R)
        Rg = sb("Rg", [P, (NG // 4) * GP * P + P * pairs_of(NG - 1)], BF16)
        Rw = sb("Rw", [P, GP * P], BF16)
        w1c = sb("w1c", [P, PAIRS])
        obias = sb("obias", [P, PAIRS])
        ident = sb("ident", [P, P])
        identb = sb("identb", [P, P], BF16)

        ps = ctx.enter_context(nc.psum_tensor("ps", [P, 8, 512], F32))

        zf = z[:, :, :].rearrange("p a b -> p (a b)")
        xf = x1[:, :, :].rearrange("p a b -> p (a b)")
        used = {"x": 0, "z": 0}

        def scratch(where, a, b=None):
            n = a * (b or 1)
            at = used[where]
            used[where] += n
            assert used[where] <= C * F
            piece = (xf if where == "x" else zf)[:, at:at + n]
            return piece.rearrange("p (a b) -> p a b", a=a) if b else piece

        Qr = scratch("z", 2 * C, NS).rearrange("p (a l) n -> p a l n", a=2)
        Qi = scratch("z", 2 * C, NS).rearrange("p (a l) n -> p a l n", a=2)
        tsb = zf[:, 0:2 * C * C].rearrange("p (a j l) -> p a j l", a=2, j=C)
        Ta = scratch("x", C, NS).rearrange("p (a l) n -> p a l n", a=2)
        Tb = scratch("x", C, NS).rearrange("p (a l) n -> p a l n", a=2)
        ldt, dsk, dt_ = (scratch("x", 2) for _ in range(3))
        lAr, Aim, Cr, Ci, eA, ah, bb, kf, ang, th, sn, sh = (scratch("x", 2, NS) for _ in range(12))
        cs, em, ea, wr, wi, t1, t2, t3 = (scratch("x", 2, NS) for _ in range(8))
        kpad = scratch("x", 2, P)
        wraw = [scratch("x", F + 1) for _ in range(4)]
        w0c, b0c, b1c = (scratch("x", PAIRS) for _ in range(3))
        WgL, WiL, WgT = scratch("x", P), scratch("x", P), scratch("x", C)
        WcL, WcT = scratch("x", 6 * C), scratch("x", 3, C)
        WoL, WoR, boL, bc2 = scratch("x", 3, F), scratch("x", 3, KR), scratch("x", 3), scratch("x", 1)
        Gb = toep[:, :, :]
        Wib = scratch("z", P)
        mA, mB = ([scratch("z", P + WIN) for h in range(2)] for _ in range(2))
        mI, mG = scratch("z", P), scratch("z", P)
        one1 = scratch("z", 2)
        Wself, Wprev = scratch("x", P), scratch("x", P)
        bg1, bi1 = scratch("x", C), scratch("x", C)
        bgrow, birow = scratch("x", 2 * GP, C), scratch("x", 2 * GP, C)
        pmask = scratch("x", 3, P)
        pm = scratch("x", 3)
        sa, sb_, sc = (turn[:, GP * P * i:GP * P * (i + 1)] for i in range(3))
        hb = [turn[:, GP * P * 3 + 256 * i:GP * P * 3 + 256 * (i + 1)].bitcast(BF16) for i in range(3)]
        kdram = nc.dram_tensor("kdram", [F, C * C], F32, kind="Internal").ap()

        xtail = nc.dram_tensor("xtail", [C * F, P], F32, kind="Internal").ap()
        ytail = nc.dram_tensor("ytail", [C * F, P], F32, kind="Internal").ap()

        s_out = sem("s_out")
        s_tail = sem("s_tail")
        s_par = sem("s_par")
        s_wts = sem("s_wts")
        s_kd = sem("s_kd")
        s_toep = sem("s_toep")
        s_zero = sem("s_zero")
        s_exp = sem("s_exp")
        s_arg = sem("s_arg")
        s_trig = sem("s_trig")
        s_kpad = sem("s_kpad")
        s_set = sem("s_set")
        s_pset = sem("s_pset")
        s_rows = sem("s_rows")
        s_wT = sem("s_wT")
        s_gb = sem("s_gb")
        s_rg = sem("s_rg")
        s_rgev = sem("s_rgev")
        s_ob = sem("s_ob")
        s_ready = sem("s_ready")
        s_x = [sem(f"s_x{i}") for i in range(len(XUNITS))]
        s_t = sem("s_t")
        s_conv = sem("s_conv")
        s_xt = sem("s_xt")
        s_gelu = sem("s_gelu")
        s_xtev = sem("s_xtev")
        s_zhi = sem("s_zhi")
        s_zr = sem("s_zr")
        s_zT = sem("s_zT")
        s_rT = sem("s_rT")
        s_zh = sem("s_zh")
        s_zrT = sem("s_zrT")
        s_zl = sem("s_zl")
        s_y = sem("s_y")
        s_sig = sem("s_sig")
        s_glu = sem("s_glu")
        s_add = sem("s_add")
        s_bn1 = sem("s_bn1")
        s_ln = sem("s_ln")
        s_std = sem("s_std")
        s_LT = sem("s_LT")
        s_Lt = sem("s_Lt")
        s_x1T = sem("s_x1T")
        s_x1h = sem("s_x1h")
        s_x1l = sem("s_x1l")
        s_gh = sem("s_gh")
        s_gl = sem("s_gl")
        s_gp = sem("s_gp")
        s_gw = sem("s_gw")
        s_gate = sem("s_gate")
        s_v = sem("s_v")
        s_bn2 = sem("s_bn2")
        s_n = sem("s_n")
        s_vT = sem("s_vT")
        s_vw = sem("s_vw")
        s_vh = sem("s_vh")
        s_vl = sem("s_vl")
        s_one = sem("s_one")
        s_o = sem("s_o")
        s_oev = sem("s_oev")
        s_st = [sem(f"s_st{i}") for i in range(OSLOTS)]
        OEV = 1

        def gate_bank(g, m):
            w = min(P, C * freqs_of(g))
            banks = ps[:, 4 + 2 * (g % 2):6 + 2 * (g % 2), :].rearrange("p b (i m c) -> p (b i) m c", i=2, m=2)
            return banks[:, 0:pairs_of(g), m, 0:w]

        def by_pair(a, g):
            return a.rearrange("p (n w) -> p n w", n=pairs_of(g))

        def conv_bank(g):
            return g % 2 if g in (2, 3) else 2 + g % 2

        block = ctx.enter_context(nc.Block())

        def unit_of(g):
            return [u for u, (slot, n) in enumerate(XUNITS) if slot <= g % XSLOTS < slot + n][0]

        def x_landed(j, g):
            return j * (32 * (NG // XSLOTS)) + 32 * (g // XSLOTS + 1)

        def out_halves(g):
            q0, n = g * GP, pairs_of(g)
            return [(max(q0, 1), n - (q0 == 0)), (q0, n)]

        def stored(j, groups):
            return j * (32 * (NG // OSLOTS)) + OEV + 32 * groups

        @block.sync
        def _(sp):
            def halves(dst, src):
                sp.dma_start(dst[:, 0, :], src[0:P, :]).then_inc(s_par, 16)
                sp.dma_start(dst[0:HR, 1, :], src[P:F, :]).then_inc(s_par, 16)

            sp.wait_ge(s_zero, 1)
            for dst, src in ((lAr, log_A_real), (Aim, A_imag), (Cr, C_re), (Ci, C_im)):
                halves(dst, src)
            for dst, src in ((ldt, log_dt), (dsk, Dskip)):
                col = src.rearrange("(h a) -> h a", a=1)
                sp.dma_start(dst[:, 0:1], col[0:P, :]).then_inc(s_par, 16)
                sp.dma_start(dst[0:HR, 1:2], col[P:F, :]).then_inc(s_par, 16)
            for dst, src in ((WgL, Wg), (WiL, Wi)):
                for h in range(2):
                    sp.dma_start(dst[0:C, C * h:C * h + C], src[:, :, 0, 0]).then_inc(s_wts, 16)
            for h in range(2):
                sp.dma_start(WcL[0:C, 3 * C * h:3 * C * h + 3 * C],
                             Wc.rearrange("o c k a -> o (c k a)")).then_inc(s_wts, 16)
            for i in range(3):
                n = min(P, O2 - i * P)
                sp.dma_start(WoL[0:n, i, :], Wout[i * P:i * P + n, :]).then_inc(s_wts, 16)
                sp.dma_start(boL[0:n, i:i + 1], bout.rearrange("(h a) -> h a", a=1)[i * P:i * P + n, :])\
                  .then_inc(s_wts, 16)
            for dst, src in zip(wraw, (w0, b0, w1, b1)):
                for h in range(2):
                    sp.dma_start(dst[64 * h:64 * h + 64, 0:F], src[0, :, :, 0]).then_inc(s_wts, 16)
            for h in range(2):
                sp.dma_start(bc2[64 * h:64 * h + 64, :], bc.rearrange("(h a) -> h a", a=1)).then_inc(s_wts, 16)
            for row, src in ((bg1, bg), (bi1, bi)):
                sp.dma_start(row[0:1, :], src.rearrange("(a h) -> a h", a=1)).then_inc(s_wts, 16)

            def load_x(src, start, row, u, r, j):
                slot, n = XUNITS[u]
                g = r * XSLOTS + slot
                nf = sum(freqs_of(g + i) for i in range(n))
                sp.wait_ge(s_xt, NG * j + g + n)
                dst = xring[:, slot:slot + n, :, :].rearrange("p s m t -> p (s m) t")
                for h in range(2):
                    m = (nf + 1 - h) // 2
                    part = bass.AP(src.tensor, start + (2 * GP * g + h) * row, [[F * row, C], [2 * row, m], [1, P]])
                    sp.dma_start(dst[64 * h:64 * h + 64, 0:m, :], part).then_inc(s_x[u], 16)

            for b in range(B):
                sp.dma_start(bass.AP(xtail.tensor, b * TAIL, [[P, C * F], [1, TAIL]]),
                             bass.AP(x.tensor, b * (C * F * T) + PER_B * P, [[T, C * F], [1, TAIL]]))\
                  .then_inc(s_tail, 16)

            sp.wait_ge(s_kpad, 1)
            sp.dma_start(kdram[0:P, :], tsb[:, 0, :, :].rearrange("p j l -> p (j l)")).then_inc(s_kd, 16)
            sp.dma_start(kdram[P:F, :], tsb[0:HR, 1, :, :].rearrange("p j l -> p (j l)")).then_inc(s_kd, 16)
            sp.wait_ge(s_kd, 32)
            sp.wait_ge(s_rg, NSUM)
            for h in range(2):
                n = PAIRS - h
                sp.dma_start(toep[64 * h:64 * h + 64, 0:n, :],
                             bass.AP(kdram.tensor, h * C * C, [[C, C], [2 * C * C, n], [1, C]]))\
                  .then_inc(s_toep, 16)

            with sp.Fori(0, B) as b:
                with sp.Fori(0, PER_B) as k:
                    for r in range(NG // XSLOTS):
                        for u in range(len(XUNITS)):
                            load_x(x, b * (C * F * T) + k * P, T, u, r, b * PER_B + k)
            sp.wait_ge(s_tail, 16 * B)
            for r in range(NG // XSLOTS):
                for u in range(len(XUNITS)):
                    load_x(xtail, 0, P, u, r, NCHUNK)
            f0 = 0
            for end in SCATTER:
                for s in range(OSLOTS):
                    sp.wait_ge(s_st[s], stored(NCHUNK, len(range(s, end, OSLOTS))))
                n = min(F, 2 * GP * end - 1) - f0
                for b in range(B):
                    sp.dma_start(bass.AP(out.tensor, b * (C * F * T) + f0 * T + PER_B * P, [[F * T, C], [T, n], [1, TAIL]]),
                                 bass.AP(ytail.tensor, f0 * P + b * TAIL, [[F * P, C], [P, n], [1, TAIL]]))\
                      .then_inc(s_out, 16)
                f0 += n
            sp.wait_ge(s_out, 16 * B * len(SCATTER))

        @block.gpsimd
        def _(pool):
            done = [0]

            def step(ins):
                done[0] += 1
                ins.then_inc(s_pset, 1)
                pool.wait_ge(s_pset, done[0])

            step(pool.memset(ident[:, :], 0.0))
            step(pool.affine_select(out=ident[:, :], in_=ident[:, :], compare_op=ALU.not_equal, fill=1.0,
                                    base=0, pattern=[[-1, P]], channel_multiplier=1))
            step(pool.tensor_copy(identb[:, :], ident[:, :]))
            step(pool.memset(half[:, :], 0.5))
            pool.wait_ge(s_ready, 1)

            def gate_low(j, g):
                at, n = GP * (g % GSLOTS), pairs_of(g)
                for h in range(2):
                    r = slice(C * h, C * h + C)
                    pool.wait_ge(s_gh, 2 * NG * j + 2 * g + h + 1)
                    pool.tensor_tensor(gates[r, GL + at:GL + at + n, r], G[r, GP * g:GP * g + n, :],
                                       gates[r, GH + at:GH + at + n, r].bitcast(F32),
                                       ALU.subtract).then_inc(s_gl, 1)
                    pool.wait_ge(s_gl, 2 * NG * j + 2 * g + h + 1)

            def chunk(j, tail):
                def low(i):
                    pool.wait_ge(s_zhi, NLG * j + i + 1)
                    pool.tensor_tensor(zr[:, (i + 1) % 2, :, HR:2 * HR], z[:, LG * i:LG * i + LG, H0:F],
                                       zr[:, (i + 1) % 2, :, 0:HR], ALU.subtract).then_inc(s_zr, 1)

                def add(s):
                    pool.wait_ge(s_glu, NSUB * j + s + 1)
                    dst = x1[:, 0:F, 2 * s:2 * s + 2]
                    pool.tensor_tensor(dst, dst, glu[s % 2].rearrange("p c f -> p f c"),
                                       ALU.add).then_inc(s_add, 1)

                low(0)
                low(1)
                for i in range(NLG):
                    if i + 2 < NLG:
                        low(i + 2)
                    add(2 * i)
                    add(2 * i + 1)
                for at in (0, LN1):
                    if at:
                        for g in range(GSLOTS, NG):
                            gate_low(j, g)
                    pool.wait_ge(s_ln, LN * j + at + 2)
                    pool.tensor_tensor(std[:, :], var_n[:, :], half[:, :], ALU.pow).then_inc(s_std, 1)
                for g in range(NG):
                    n = pairs_of(g)
                    pool.wait_ge(s_vh, NG * j + g + 1)
                    pool.tensor_tensor(vl[:, g % VSLOTS, 0:n, :], vw[:, g % 2, 0:n, :],
                                       vh[:, g % VSLOTS, 0:n, :].bitcast(F32), ALU.subtract).then_inc(s_vl, 1)
                    if not tail and g in GATE_AT:
                        gate_low(j + 1, GATE_AT.index(g))

            for g in range(GSLOTS):
                gate_low(0, g)
            with pool.Fori(0, NCHUNK) as j:
                chunk(j, False)
            chunk(NCHUNK, True)

        @block.scalar
        def _(act):
            act.wait_ge(s_par, 12 * 16)
            act.activation(dt_, ldt, ACT.Exp).then_inc(s_exp, 1)
            act.activation(eA, lAr, ACT.Exp).then_inc(s_exp, 1)
            act.wait_ge(s_arg, 1)
            act.activation(th, ah, ACT.Tanh).then_inc(s_trig, 1)
            act.activation(sn, ang, ACT.Sin).then_inc(s_trig, 1)
            act.activation(sh, ang, ACT.Sin, scale=0.5).then_inc(s_trig, 1)
            act.wait_ge(s_ready, 1)

            def gelu(j, g):
                nf = freqs_of(g)
                act.wait_ge(s_conv, NG * j + g + 1)
                act.activation(z[:, :, 2 * GP * g:2 * GP * g + nf],
                               ps[:, conv_bank(g), 0:C * nf].rearrange("p (h l) -> p l h", h=nf),
                               ACT.Gelu).then_inc(s_gelu, 1)

            def x_tokens(j, g):
                nf = freqs_of(g)
                act.wait_ge(s_xt, NG * j + g + 1 + XSLOTS)
                act.activation(xf[:, 2 * GP * C * g:2 * GP * C * g + C * nf], ps[:, 6 + g % 2, 0:C * nf],
                               ACT.Copy).then_inc(s_xtev, 1)

            def store(b, k, g):
                j = NCHUNK if b is None else b * PER_B + k
                act.wait_ge(s_oev, NG * j + g + 1 + OEV)
                for h, (q, n) in enumerate(out_halves(g)):
                    src = oring[64 * h:64 * h + 64, g % OSLOTS, q - GP * g:q - GP * g + n, :]
                    f0 = 2 * q - 1 + h
                    if b is not None:
                        dst = bass.AP(out.tensor, b * (C * F * T) + k * P + f0 * T, [[F * T, C], [2 * T, n], [1, P]])
                    else:
                        dst = bass.AP(ytail.tensor, f0 * P, [[F * P, C], [2 * P, n], [1, P]])
                    act.dma_start(dst, src).then_inc(s_st[g % OSLOTS], 16)

            def gate_high(j, g):
                at, n = GH + GP * (g % GSLOTS), pairs_of(g)
                for h in range(2):
                    r = slice(C * h, C * h + C)
                    act.activation(gates[r, at:at + n, r], G[r, GP * g:GP * g + n, :], ACT.Copy).then_inc(s_gh, 1)

            def mixing(j, still=None):
                def sigmoid(s):
                    act.wait_ge(s_y, NSUB * j + s + 1)
                    if s >= 2:
                        act.wait_ge(s_glu, NSUB * j + s - 1)
                    bank = 6 - 2 * (s % 2)
                    act.activation(sig[:, s % 2, :, :], ps[:, bank:bank + 2, F:O2], ACT.Sigmoid).then_inc(s_sig, 1)

                def last_parts(i):
                    if i >= 2:
                        act.wait_ge(s_rT, NLG * j + i - 1)
                    src = z[:, LG * i:LG * i + LG, H0:F]
                    if i == 0:
                        act.wait_ge(s_gelu, NG * j + NG)
                    act.activation(zr[:, (i + 1) % 2, :, 0:HR].bitcast(F32R), src, ACT.Copy)
                    act.activation(zr[:, (i + 1) % 2, :, 2 * HR:3 * HR], src, ACT.Copy).then_inc(s_zhi, 1)

                last_parts(0)
                act.wait_ge(s_vl, NG * j + OEV)
                last_parts(1)
                for i in range(NLG + 1):
                    if i < NLG:
                        act.wait_ge(s_zT, NLG * j + i + 1)
                        if i >= 2:
                            act.wait_ge(s_y, NSUB * j + 2 * i - 2)
                        act.activation(zh[:, i % 2, :, :], ps[:, 2 + i % 2, :].rearrange("p (l t) -> p l t", l=LG),
                                       ACT.Copy).then_inc(s_zh, 1)
                        act.wait_ge(s_rT, NLG * j + i + 1)
                        act.activation(zrT[0:KR, i % 2, :, :],
                                       ps[0:KR, i % 2, :].rearrange("p (l t) -> p l t", l=LG),
                                       ACT.Copy).then_inc(s_zrT, 1)
                        if i + 2 < NLG:
                            last_parts(i + 2)
                    if still and i < SLAG:
                        store(*still, NG - SLAG + i)
                    if i >= 1:
                        sigmoid(2 * i - 2)
                        sigmoid(2 * i - 1)

            def gating(j):
                def x1_high(g):
                    n = pairs_of(g)
                    act.wait_ge(s_x1T, NG * j + g + 1)
                    if g >= 2:
                        act.wait_ge(s_gp, NG * j + g - 1)
                    act.activation(x1h[:, g % 2, 0:n, :], ps[:, g % 2, 0:P * n].rearrange("p (n t) -> p n t", n=n),
                                   ACT.Copy).then_inc(s_x1h, 1)

                def gate_of(q):
                    w = C * freqs_of(q)
                    act.wait_ge(s_gw, NG * j + q + 1)
                    if q >= 2:
                        act.wait_ge(s_v, NG * j + q - 1)
                    act.activation(by_pair(gate[:, q % 2, 0:w], q), gate_bank(q, 0), ACT.Sigmoid,
                                   scale=rstd[:, 0:1]).then_inc(s_gate, 1)

                for s in range(OSLOTS):
                    act.wait_ge(s_st[s], stored(j, 0))
                x1_high(0)
                x1_high(1)
                for g in range(2, NG + 2):
                    if g < NG:
                        x1_high(g)
                    gate_of(g - 2)
                    if g - 2 + GSLOTS < NG:
                        gate_high(j, g - 2 + GSLOTS)

            def last_phase(b, k):
                j = NCHUNK if b is None else b * PER_B + k
                early = EARLY if b is not None else 0

                def high(g):
                    n = pairs_of(g)
                    act.wait_ge(s_vw, NG * j + g + 1)
                    if g >= VSLOTS:
                        act.wait_ge(s_o, NG * j + g - VSLOTS + 2)
                    act.activation(vh[:, g % VSLOTS, 0:n, :], vw[:, g % 2, 0:n, :], ACT.Copy).then_inc(s_vh, 1)

                for g in range(early - 1):
                    gelu(j + 1, g)
                for g in range(NG):
                    high(g)
                    if early and g in GATE_AT:
                        gate_high(j + 1, GATE_AT.index(g))
                    if early and g >= 1:
                        x_tokens(j + 1, g - 1)
                    if early and early - 1 <= g + LEAD - 1 < NG:
                        gelu(j + 1, g + LEAD - 1)
                    if early and g + LEAD - 1 == NG - 1:
                        act.activation(spare[:, :], half[:, :], ACT.Sigmoid)
                    if g >= SLAG:
                        store(b, k, g - SLAG)
                if early:
                    x_tokens(j + 1, NG - 1)
                if b is None:
                    for g in range(NG - SLAG, NG):
                        store(b, k, g)

            for g in range(GSLOTS):
                gate_high(0, g)
            for g in range(NG):
                gelu(0, g)
                x_tokens(0, g)
            mixing(0)
            with act.Fori(0, B) as b:
                with act.Fori(0, PER_B) as k:
                    j = b * PER_B + k
                    gating(j)
                    last_phase(b, k)
                    mixing(j + 1, (b, k))
            gating(NCHUNK)
            last_phase(None, None)

        @block.tensor
        def _(pe):
            pe.wait_ge(s_pset, 4)
            pe.wait_ge(s_rows, 1)
            pe.transpose(ps[:, 0, 0:C], WgL[0:C, :], ident[0:C, 0:C])
            pe.transpose(ps[:, 0, C:2 * C], WiL[0:C, :], ident[0:C, 0:C])
            for k in range(3):
                pe.transpose(ps[:, 1, C * k:C * k + C], WcL[0:C, :].rearrange("o (c k) -> o k c", k=3)[:, k, :],
                             ident[0:C, 0:C])
            for i in range(3):
                n = min(P, O2 - i * P)
                pe.transpose(ps[:, 2, i * P:i * P + n], WoL[0:n, i, 0:H0], ident[0:n, 0:n])
                pe.transpose(ps[0:KR, 3, i * P:i * P + n], WoR[0:n, i, :], ident[0:n, 0:n])
            for i in range(3):
                pe.matmul(ps[:, 4, 2 * i:2 * i + 2], pmask[0:1, i, :], one1[0:1, :], start=True, stop=True)
            pe.matmul(ps[:, 5, :], mI[0:1, :], birow[0:1, :, :].rearrange("p a b -> p (a b)"), start=True,
                      stop=True).then_inc(s_wT, 1)
            pe.wait_ge(s_gb, 2)
            for s in range(NSUM):
                groups = range(4 * s, min(4 * s + 4, NG))
                n = pairs_of(groups[0])
                pe.matmul(ps[:, SUM_BANKS[s], 0:P * n], mG[0:1, :],
                          bgrow[0:1, 0:2 * n, :].rearrange("p a b -> p (a b)"),
                          start=True, stop=False, skip_group_check=True)
                for g in groups:
                    n = pairs_of(g)
                    o = ps[:, SUM_BANKS[s], 0:P * n]
                    at = WIN - 32 * (g % 4)
                    for mask, factor in ((mA, G), (mB, Gb)):
                        for h in range(2):
                            ins = pe.matmul(o.rearrange("p (n h c) -> p n h c", n=n, h=2)[:, :, h, :],
                                            mask[h][:, at:at + P], factor[:, GP * g:GP * g + n, :],
                                            start=False, stop=(g == groups[-1] and factor is Gb and h == 1),
                                            skip_group_check=True)
                ins.then_inc(s_rg, 1)
            pe.matmul(ps[:, 0, 0:PAIRS], Wself[:, :], b1c, start=True, stop=False, skip_group_check=True)
            pe.matmul(ps[:, 0, 1:PAIRS], Wprev[:, :], b1c[:, 0:PAIRS - 1], start=False, stop=True,
                      skip_group_check=True).then_inc(s_ob, 1)
            pe.wait_ge(s_ready, 1)

            def s4d(j, g):
                pe.wait_ge(s_t, 2 * NG * j + 2 * g + 2)
                pe.wait_ge(s_x[unit_of(g)], x_landed(j, g))
                if g >= 4:
                    pe.wait_ge(s_gelu, NG * j + (g - 1 if g >= 6 else g - 3))
                for i in range(pairs_of(g)):
                    ins = pe.matmul(ps[:, conv_bank(g), P * i:P * i + P], xring[:, g % XSLOTS, i, :],
                                    tring[:, g % 3, i, :], start=True, stop=True)
                ins.then_inc(s_conv, 1)

            def x_tokens(j, g):
                if g >= 2:
                    pe.wait_ge(s_xtev, NG * j + g - 1)
                for i in range(pairs_of(g)):
                    ins = pe.transpose(ps[:, 6 + g % 2, P * i:P * i + P], xring[:, g % XSLOTS, i, :], ident[:, :])
                ins.then_inc(s_xt, 1)

            def chunk(j, tail):
                pe.wait_ge(s_gelu, NG * j + NG)
                for i in range(NLG + 1):
                    if i < NLG:
                        if i >= 2:
                            pe.wait_ge(s_zl, NLG * j + i - 1)
                        for c in range(LG):
                            ins = pe.transpose(ps[:, 2 + i % 2, P * c:P * c + P], z[:, LG * i + c, 0:H0], ident[:, :])
                        ins.then_inc(s_zT, 1)
                        pe.wait_ge(s_zr, NLG * j + i + 1)
                        if i == 1:
                            pe.wait_ge(s_one, j + 1)
                        if i >= 2:
                            pe.wait_ge(s_zrT, NLG * j + i - 1)
                        for c in range(LG):
                            ins = pe.transpose(ps[0:KR, i % 2, P * c:P * c + P], zr[:, (i + 1) % 2, c, :],
                                               ident[:, :])
                        ins.then_inc(s_rT, 1)
                    if i >= 1:
                        k = (i - 1) % 2
                        pe.wait_ge(s_zl, NLG * j + i)
                        for s in (2 * i - 2, 2 * i - 1):
                            if s == 0:
                                pe.wait_ge(s_xtev, NG * j + NG)
                            if s == 1:
                                pe.wait_ge(s_oev, NG * j + OEV)
                            if s >= 2:
                                pe.wait_ge(s_glu, NSUB * j + s - 1)
                            for c in range(2):
                                o = ps[:, 6 - 2 * (s % 2) + c, 0:O2]
                                l = 2 * (s % 2) + c
                                pe.matmul(o, zh[:, k, l, :], Wh[:, :], start=True, stop=False)
                                pe.matmul(o, zh[:, k, l, :], Wl[:, :], start=False, stop=False)
                                pe.matmul(o, zl[:, k, l, :], Wh[:, :], start=False, stop=False)
                                if l == 0:
                                    pe.wait_ge(s_zrT, NLG * j + i)
                                ins = pe.matmul(o, zrT[0:KR, k, l, :], Wr[:, :], start=False, stop=True)
                            ins.then_inc(s_y, 1)
                early = EARLY if not tail else 0
                for g in range(min(early, 2)):
                    s4d(j + 1, g)
                pe.wait_ge(s_add, NSUB * j + NSUB)
                def x1_channels(g):
                    if g >= 2:
                        pe.wait_ge(s_x1l, NG * j + g - 1)
                    for i in range(pairs_of(g)):
                        f = 2 * (GP * g + i)
                        ins = pe.transpose(ps[:, g % 2, P * i:P * i + P], xf[:, C * f:C * f + P], ident[:, :])
                    ins.then_inc(s_x1T, 1)

                def gate_products(k):
                    pe.wait_ge(s_x1l, NG * j + k + 1)
                    pe.wait_ge(s_gl, 2 * NG * j + 2 * k + 2)
                    if k == 0:
                        pe.wait_ge(s_glu, NSUB * j + NSUB)
                    if k >= 2:
                        pe.wait_ge(s_v, NG * j + k - 1)
                    for i in range(pairs_of(k)):
                        o = ps[:, 4 + 2 * (k % 2) + i // 2, 2 * P * (i % 2):2 * P * (i % 2) + 2 * P]
                        at = GP * (k % GSLOTS) + i
                        high = gates[:, GH + at:WIH + 1:WIH - GH - at, :]
                        low = gates[:, GL + at:WIL + 1:WIL - GL - at, :]
                        pe.matmul(o, x1h[:, k % 2, i, :], high, start=(i % 2 == 0), stop=False, skip_group_check=True)
                        pe.matmul(o, x1h[:, k % 2, i, :], low, start=False, stop=False, skip_group_check=True)
                        ins = pe.matmul(o, x1l[:, k % 2, i, :], high, start=False, stop=False,
                                        skip_group_check=True)
                    ins.then_inc(s_gp, 1)

                def rank_one(k):
                    for i in range(0, pairs_of(k), 2):
                        n = min(2, pairs_of(k) - i)
                        o = ps[:, 4 + 2 * (k % 2) + i // 2, :].rearrange("p (i m c) -> p i m c", i=2, m=2)
                        at = GP * P * (k // 4) + P * i
                        pe.matmul(o[:, 0:n, 0, :], Lt[:, k % 4, :], Rg[:, at:at + P * n],
                                  start=False, stop=False, skip_group_check=True)
                        ins = pe.matmul(o[:, 0:n, 1, :], Lt[:, 0, :], Rw[:, 0:P * n],
                                        start=False, stop=True, skip_group_check=True)
                    ins.then_inc(s_gw, 1)

                x1_channels(0)
                x1_channels(1)
                gate_products(0)
                gate_products(1)
                x1_channels(2)
                pe.wait_ge(s_ln, LN * j + LN1 - 1)
                for q in range(4):
                    at = WIN - 32 * q
                    ins = pe.transpose(ps[:, 1, 0:256].bitcast(BF16)[:, P * q:P * q + P],
                                       Lsrc[:, at:at + P], identb[:, :])
                ins.then_inc(s_LT, 1)
                pe.wait_ge(s_Lt, j + 1)
                rank_one(0)
                rank_one(1)
                for k in range(2, NG):
                    if k + 1 < NG:
                        x1_channels(k + 1)
                    gate_products(k)
                    rank_one(k)
                def v_channels(g):
                    pe.wait_ge(s_n, NG * j + g + 1)
                    if g >= 2:
                        pe.wait_ge(s_vw, NG * j + g - 1)
                    for i in range(pairs_of(g)):
                        f = 2 * (GP * g + i)
                        ins = pe.transpose(ps[:, g % 2, P * i:P * i + P], xf[:, C * f:C * f + P], ident[:, :])
                    ins.then_inc(s_vT, 1)

                def conv(k):
                    n = pairs_of(k)
                    pe.wait_ge(s_vl, NG * j + k + 1 + OEV)
                    if k >= 2:
                        pe.wait_ge(s_oev, NG * j + k - 1 + OEV)
                    o = ps[:, 4 + k % 2, :]
                    now, last = k % VSLOTS, (k - 1) % VSLOTS
                    work = []
                    for hl, (v, ws, wp) in enumerate(((vh, Wself_h, Wprev_h), (vh, Wself_l, Wprev_l),
                                                      (vl, Wself_h, Wprev_h))):
                        work.append((o[:, 0:P * n], ws, v[:, now, 0:n, :]))
                        if k > 0:
                            work.append((o[:, 0:P], wp, v[:, last, GP - 1:GP, :]))
                        if n > 1:
                            work.append((o[:, P:P * n], wp, v[:, now, 0:n - 1, :]))
                    for m, (cols, w, v) in enumerate(work):
                        ins = pe.matmul(cols, w[:, :], v.rearrange("p n t -> p (n t)"), start=(m == 0),
                                        stop=(m == len(work) - 1), skip_group_check=True)
                    ins.then_inc(s_o, 1)

                if early:
                    pe.wait_ge(s_x1l, NG * j + NG)
                for g in range(2, early - 1):
                    s4d(j + 1, g)
                if early:
                    pe.wait_ge(s_gelu, NG * (j + 1) + 4)
                v_channels(0)
                v_channels(1)
                for g in range(1, NG + 2):
                    if 2 <= g < NG:
                        v_channels(g)
                    if early and g == 1:
                        s4d(j + 1, early - 1)
                    if early <= g + LEAD < NG and early:
                        s4d(j + 1, g + LEAD)
                    if early and g <= NG:
                        x_tokens(j + 1, g - 1)
                    if g >= 2:
                        conv(g - 2)

            for g in range(NG):
                s4d(0, g)
                x_tokens(0, g)
            with pe.Fori(0, NCHUNK) as j:
                chunk(j, False)
            chunk(NCHUNK, True)

        @block.vector
        def _(dve):
            done = [0]

            def step(ins):
                done[0] += 1
                ins.then_inc(s_set, 1)
                dve.wait_ge(s_set, done[0])

            def tt(o, a, b, op):
                step(dve.tensor_tensor(o, a, b, op))

            def ts(o, a, s1, s2, op0, op1=ALU.bypass):
                step(dve.tensor_scalar(o, a, s1, s2, op0, op1) if s2 is not None
                     else dve.tensor_scalar(o, a, s1, None, op0))

            def stt(o, a, s, b, op0, op1):
                step(dve.scalar_tensor_tensor(out=o, in0=a, scalar=s, in1=b, op0=op0, op1=op1))

            add, sub, mul = ALU.add, ALU.subtract, ALU.mult
            dve.memset(xf, 0.0).then_inc(s_zero, 1)
            step(dve.memset(zf, 0.0))
            step(dve.memset(tring[:, :, :, :], 0.0))
            step(dve.tensor_copy(gates[:, 0:WIH, :].rearrange("p a b -> p (a b)"), zf[:, 0:WIH * P]))
            for m in (Lsrc, w1c):
                step(dve.memset(m[:, :], 0.0))
            step(dve.memset(Lsrc[:, WIN + K_ONE:WIN + K_ONE + 3], 1.0))
            for h in range(2):
                r = slice(C * h, C * h + C)
                step(dve.memset(mA[h][r, WIN + K_MEAN:WIN + K_MEAN + NSP], -1.0))
                step(dve.memset(mB[h][r, WIN + K_STD:WIN + K_STD + NSP], 1.0))
            step(dve.memset(mI[:, K_ONE:K_ONE + 3], 1.0))
            step(dve.memset(mG.rearrange("p (q k) -> p q k", q=4)[:, :, K_STD:K_STD + NSP], 1.0))
            step(dve.memset(one1, 1.0))
            dve.memset(ms[:, :], 0.0).then_inc(s_xt, XSLOTS)
            dve.memset(rstd[:, :], 0.0).then_inc(s_oev, OEV)
            dve.memset(nmr[:, :], 0.0).then_inc(s_vl, OEV)
            dve.wait_ge(s_vl, OEV)
            for s in s_st:
                dve.memset(res[:, :], 0.0).then_inc(s, OEV)
                dve.wait_ge(s, OEV)
            dve.wait_ge(s_oev, OEV)
            dve.wait_ge(s_zero, 1)
            for k, part in [(K_MEAN + i, r) for i, (_, r) in enumerate(SPLITS)]\
                    + [(K_STD + i, r) for i, (_, r) in enumerate(SPLITS)] + [(K_ONE + i, i) for i in range(3)]:
                step(dve.memset(pmask[0:1, part, :].rearrange("p (q k) -> p q k", q=4)[:, :, k], 1.0))

            dve.wait_ge(s_exp, 2)
            dtb = dt_.unsqueeze(2).to_broadcast([P, 2, NS])
            tt(t1, eA, dtb, mul)
            ts(ah, t1, -0.5, None, mul)
            tt(bb, Aim, dtb, mul)
            magic = 12582912.0
            ts(kf, bb, 1.0 / TWO_PI, magic, mul, add)
            ts(t1, kf, magic, None, sub)
            rest = TWO_PI
            c1 = 6.28125
            c2 = 0.0019350051879882812
            c3 = rest - c1 - c2
            stt(t2, t1, -c1, bb, mul, add)
            stt(t3, t1, -c2, t2, mul, add)
            stt(t2, t1, -c3, t3, mul, add)
            dve.tensor_scalar(ang, t2, 3.1415925, -3.1415925, ALU.min, ALU.max).then_inc(s_arg, 1)
            dve.wait_ge(s_trig, 3)
            tt(t1, sh, sh, mul)
            ts(t1, t1, -2.0, None, mul)
            ts(cs, t1, 1.0, None, add)
            ts(t2, th, -1.0, 1.0, mul, add)
            step(dve.reciprocal(t3, t2))
            tt(t2, th, t3, mul)
            ts(em, t2, 2.0, None, mul)
            ts(ea, em, 1.0, None, add)
            tt(wr, ea, cs, mul)
            tt(wi, ea, sn, mul)
            tt(t2, em, cs, mul)
            tt(em, t2, t1, add)
            ts(eA, eA, -1.0, None, mul)
            tt(t1, Cr, em, mul)
            tt(t2, Ci, wi, mul)
            tt(t3, t1, t2, sub)
            tt(t1, Cr, wi, mul)
            tt(t2, Ci, em, mul)
            tt(cs, t1, t2, add)
            tt(t1, eA, eA, mul)
            tt(t2, Aim, Aim, mul)
            tt(t1, t1, t2, add)
            step(dve.reciprocal(t2, t1))
            ts(t2, t2, 2.0, None, mul)
            tt(t1, t3, eA, mul)
            tt(ea, cs, Aim, mul)
            tt(t1, t1, ea, add)
            tt(Qr[:, :, 0, :], t1, t2, mul)
            tt(t1, cs, eA, mul)
            tt(ea, t3, Aim, mul)
            tt(t1, t1, ea, sub)
            tt(Qi[:, :, 0, :], t1, t2, mul)
            dve.wait_ge(s_wts, 16 * 24)
            last = WoL[:, :, H0:F]
            step(dve.tensor_copy(WoR[:, :, 0:HR].bitcast(F32R), last))
            step(dve.tensor_copy(WoR[:, :, HR:2 * HR].bitcast(F32R), last))
            tt(WoR[:, :, 2 * HR:3 * HR], last, WoR[:, :, 0:HR], sub)
            step(dve.tensor_copy(WoR[:, :, 3 * HR].bitcast(F32R), boL))
            tt(WoR[:, :, 3 * HR + 1], boL, WoR[:, :, 3 * HR], sub)
            for row, src in ((bgrow, bg1), (birow, bi1)):
                step(dve.tensor_copy(row[0:1, :, :], src[0:1, :].unsqueeze(1).to_broadcast([1, 2 * GP, C])))
            for dst, src in zip((w0c, b0c, w1c[:, :], b1c), wraw):
                step(dve.tensor_copy(dst[0:C, :], src[0:C, 0:F:2]))
                step(dve.tensor_copy(dst[C:P, 0:PAIRS - 1], src[C:P, 1:F:2]))
            dve.memset(mv[:, :], 0.0).then_inc(s_rows, 1)
            dve.wait_ge(s_wT, 1)
            step(dve.tensor_copy(WgT, ps[:, 0, 0:C]))
            for h in range(2):
                r = slice(C * h, C * h + C)
                step(dve.tensor_copy(Wib[r, r], ps[r, 0, C:2 * C]))
                step(dve.tensor_copy(Wself[r, C:P], ps[r, 1, C * (1 + h):C * (2 + h)]))
                step(dve.tensor_copy(Wprev[r, 0:C], ps[r, 1, C * h:C * h + C]))
            step(dve.tensor_copy(Wself[0:C, 0:C], ps[0:C, 1, 2 * C:3 * C]))
            step(dve.tensor_copy(Wprev[C:P, C:P], ps[C:P, 1, 0:C]))
            for w, w_h, w_l in ((Wself, Wself_h, Wself_l), (Wprev, Wprev_h, Wprev_l)):
                step(dve.tensor_copy(w_h[:, :], w[:, :]))
                tt(w_l[:, :], w[:, :], w_h[:, :].bitcast(F32), sub)
            step(dve.tensor_copy(Wh[:, :], ps[:, 2, 0:O2]))
            tt(Wl[:, :], ps[:, 2, 0:O2], Wh[:, :].bitcast(F32), sub)
            step(dve.tensor_copy(Wr[:, :], ps[0:KR, 3, 0:O2]))
            step(dve.tensor_copy(pm, ps[:, 4, 0:6:2]))
            step(dve.tensor_copy(gates[:, WIH, :], Wib))
            tt(gates[:, WIL, :], Wib, gates[:, WIH, :].bitcast(F32), sub)
            for dst, w in ((G[:, :, :], w0c), (Gb, b0c)):
                dve.tensor_tensor(dst, WgT.unsqueeze(1).to_broadcast([P, PAIRS, C]),
                                  w.unsqueeze(2).to_broadcast([P, PAIRS, C]), mul).then_inc(s_gb, 1)

            s = 1
            while s < C:
                wrb = wr.unsqueeze(2).to_broadcast([P, 2, s, NS])
                wib = wi.unsqueeze(2).to_broadcast([P, 2, s, NS])
                lo_r, lo_i, hi_r, hi_i = Qr[:, :, 0:s], Qi[:, :, 0:s], Qr[:, :, s:2 * s], Qi[:, :, s:2 * s]
                tt(Ta[:, :, 0:s], lo_r, wrb, mul)
                tt(Tb[:, :, 0:s], lo_i, wib, mul)
                tt(hi_r, Ta[:, :, 0:s], Tb[:, :, 0:s], sub)
                if 2 * s < C:
                    tt(Ta[:, :, 0:s], lo_r, wib, mul)
                    tt(Tb[:, :, 0:s], lo_i, wrb, mul)
                    tt(hi_i, Ta[:, :, 0:s], Tb[:, :, 0:s], add)
                    tt(t1, wr, wr, mul)
                    tt(t2, wi, wi, mul)
                    tt(t3, wr, wi, mul)
                    tt(wr, t1, t2, sub)
                    ts(wi, t3, 2.0, None, mul)
                s *= 2
            step(dve.tensor_reduce(kpad[:, :, C - 1:2 * C - 1], Qr, AX.X, add))
            k0 = kpad[:, :, C - 1]
            tt(k0, k0, dsk, add)
            for i in range(C):
                ins = dve.tensor_copy(tsb[:, :, i, :], kpad[:, :, C - 1 - i:2 * C - 1 - i])
            ins.then_inc(s_kpad, 1)

            def split(bank, w, dst):
                src = ps[:, bank, 0:w]
                step(dve.tensor_copy(hb[0][:, 0:w], src))
                tt(sa[:, 0:w], src, hb[0][:, 0:w], sub)
                step(dve.tensor_copy(hb[1][:, 0:w], sa[:, 0:w]))
                tt(sb_[:, 0:w], sa[:, 0:w], hb[1][:, 0:w], sub)
                step(dve.tensor_copy(hb[2][:, 0:w], sb_[:, 0:w]))
                ts(sa[:, 0:w], hb[0][:, 0:w], pm[:, 0:1], None, mul)
                stt(sc[:, 0:w], hb[1][:, 0:w], pm[:, 1:2], sa[:, 0:w], mul, add)
                return dve.scalar_tensor_tensor(out=dst, in0=hb[2][:, 0:w], scalar=pm[:, 2:3], in1=sc[:, 0:w],
                                                op0=mul, op1=add)

            step(split(5, P * GP, Rw[:, :]))
            dve.wait_ge(s_rg, NSUM)
            step(dve.memset(toep[64:P, PAIRS - 1, :], 0.0))
            for k in range(NSUM):
                w = P * GP if 4 * k + 3 < NG else P * pairs_of(NG - 1)
                split(SUM_BANKS[k], w, Rg[:, GP * P * k:GP * P * k + w]).then_inc(s_rgev, 1)
                dve.wait_ge(s_rgev, k + 1)
            dve.wait_ge(s_ob, 1)
            ts(obias[:, :], ps[:, 0, 0:PAIRS], bc2, None, add)
            step(dve.memset(zr[:, 1, :, 3 * HR:KR], 1.0))
            dve.memset(xf[:, C * F:], 0.0).then_inc(s_ready, 1)
            dve.wait_ge(s_ready, 1)
            dve.wait_ge(s_toep, 32)

            def toeplitz(j, g):
                n = pairs_of(g)
                if g >= 3:
                    dve.wait_ge(s_conv, NG * j + g - 2)
                for h in range(2):
                    dve.tensor_copy(tring[64 * h:64 * h + 64, g % 3, 0:n, 64 * h:64 * h + 64],
                                    toep[64 * h:64 * h + 64, GP * g:GP * g + n, :]).then_inc(s_t, 1)

            def chunk(j, tail):
                early = EARLY if not tail else 0
                def bn1(s):
                    dve.wait_ge(s_add, NSUB * j + s + 1)
                    dve.bn_stats(stats[:, s, :], x1[:, 0:F, 2 * s:2 * s + 2]).then_inc(s_bn1, 1)

                for i in range(NLG + 1):
                    if i < NLG:
                        dve.wait_ge(s_zh, NLG * j + i + 1)
                        if i >= 2:
                            dve.wait_ge(s_y, NSUB * j + 2 * i - 2)
                        dve.tensor_tensor(zl[:, i % 2, :, :], ps[:, 2 + i % 2, :].rearrange("p (l t) -> p l t", l=LG),
                                          zh[:, i % 2, :, :].bitcast(F32), sub).then_inc(s_zl, 1)
                    if i == 1:
                        dve.wait_ge(s_st[0], stored(j, 0))
                    if 4 <= i < 4 + min(early, 3):
                        toeplitz(j + 1, i - 4)
                    if i >= 1:
                        for s in (2 * i - 2, 2 * i - 1):
                            dve.wait_ge(s_sig, NSUB * j + s + 1)
                            if s >= 2:
                                dve.wait_ge(s_add, NSUB * j + s - 1)
                            bank = 6 - 2 * (s % 2)
                            dve.tensor_tensor(glu[s % 2], ps[:, bank:bank + 2, 0:F], sig[:, s % 2, :, :],
                                              mul).then_inc(s_glu, 1)
                            if s >= 2:
                                bn1(s - 2)
                bn1(NSUB - 2)
                bn1(NSUB - 1)

                at = [LN * j]

                def ln_step(ins):
                    at[0] = at[0] + 1
                    ins.then_inc(s_ln, 1)
                    dve.wait_ge(s_ln, at[0])

                def x1_low(g):
                    n = pairs_of(g)
                    dve.wait_ge(s_x1h, NG * j + g + 1)
                    dve.tensor_tensor(x1l[:, g % 2, 0:n, :], ps[:, g % 2, 0:P * n].rearrange("p (n t) -> p n t", n=n),
                                      x1h[:, g % 2, 0:n, :].bitcast(F32), sub).then_inc(s_x1l, 1)

                def std_of(nstats, roots, meanwhile=None):
                    ln_step(dve.bn_aggr(mv[:, :], stats[:, 0:nstats, :]))
                    ln_step(dve.tensor_scalar(var_n[:, :], mv[:, 1:2], float(NTOT) / (NTOT - 1), None, mul))
                    if meanwhile:
                        meanwhile()
                    dve.wait_ge(s_std, roots)
                    ln_step(dve.tensor_scalar(ms[:, 1:2], std[:, :], 1e-8, None, add))

                dve.wait_ge(s_ready, 1)
                dve.wait_ge(s_bn1, NSUB * j + NSUB)
                std_of(NSUB, 2 * j + 1, lambda: (ln_step(dve.tensor_copy(ms[:, 0:1], mv[:, 0:1])), x1_low(0), x1_low(1)))
                fac = Lsrc[:, WIN:WIN + 2 * NSP].rearrange("p (m k) -> p m k", m=2)
                rest = ms[:, :]
                for part in range(3):
                    ks = [k for k, (lp, _) in enumerate(SPLITS) if lp == part]
                    ln_step(dve.tensor_copy(fac[:, :, ks[0]:ks[-1] + 1],
                                            rest.unsqueeze(2).to_broadcast([P, 2, len(ks)])))
                    if part < 2:
                        ln_step(dve.tensor_tensor(res[:, :], rest, fac[:, :, ks[0]], sub))
                        rest = res[:, :]
                ln_step(dve.reciprocal(rstd[:, :], ms[:, 1:2]))

                dve.wait_ge(s_LT, j + 1)
                dve.tensor_copy(Lt[:, :, :].rearrange("p q t -> p (q t)"), ps[:, 1, 0:256].bitcast(BF16))\
                   .then_inc(s_Lt, 1)

                def bn2(g):
                    dve.wait_ge(s_v, NG * j + g + 1)
                    v = xf[:, 2 * GP * C * g:2 * GP * C * g + C * freqs_of(g)]
                    dve.bn_stats(stats[:, g, :], v).then_inc(s_bn2, 1)

                for g in range(NG):
                    if early and g in (1, 2):
                        toeplitz(j + 1, g + 2)
                    if g + 2 < NG:
                        x1_low(g + 2)
                    w = C * freqs_of(g)
                    dve.wait_ge(s_gate, NG * j + g + 1)
                    dve.tensor_tensor(by_pair(xf[:, 2 * GP * C * g:2 * GP * C * g + w], g), gate_bank(g, 1),
                                      by_pair(gate[:, g % 2, 0:w], g), mul).then_inc(s_v, 1)
                    if 1 <= g < NG - 1:
                        bn2(g - 1)
                for g in range(NG - 2, NG):
                    bn2(g)
                dve.wait_ge(s_ready, 1)
                dve.wait_ge(s_bn2, NG * j + NG)
                std_of(NG, 2 * j + 2, (lambda: toeplitz(j + 1, 5)) if early else None)
                ln_step(dve.reciprocal(rstd[:, :], ms[:, 1:2]))
                ln_step(dve.tensor_scalar(nmr[:, :], mv[:, 0:1], rstd[:, 0:1], -1.0, mul, mul))

                def norm(g):
                    v = xf[:, 2 * GP * C * g:2 * GP * C * g + C * freqs_of(g)]
                    dve.tensor_scalar(v, v, rstd[:, 0:1], nmr[:, 0:1], mul, add).then_inc(s_n, 1)

                norm(0)
                norm(1)
                for g in range(NG + 3):
                    if g < NG:
                        n = pairs_of(g)
                        dve.wait_ge(s_vT, NG * j + g + 1)
                        if g >= 2:
                            dve.wait_ge(s_vl, NG * j + g - 1 + OEV)
                        dve.tensor_tensor(vw[:, g % 2, 0:n, :], ps[:, g % 2, 0:P * n].rearrange("p (n t) -> p n t", n=n),
                                          w1c[:, GP * g:GP * g + n].unsqueeze(2).to_broadcast([P, n, P]),
                                          mul).then_inc(s_vw, 1)
                        if g + 2 < NG:
                            norm(g + 2)
                    if early and g == 0:
                        toeplitz(j + 1, early - 1)
                    if early and early <= g + LEAD + 1 < NG:
                        toeplitz(j + 1, g + LEAD + 1)
                    if early and g == NG + 2:
                        dve.wait_ge(s_vl, NG * j + NG + OEV)
                        dve.memset(zr[:, 0, :, 3 * HR:KR], 1.0).then_inc(s_one, 1)
                    if g >= 3:
                        q = g - 3
                        n = pairs_of(q)
                        dve.wait_ge(s_o, NG * j + q + 1)
                        dve.wait_ge(s_st[q % OSLOTS], stored(j, q // OSLOTS))
                        dve.tensor_tensor(oring[:, q % OSLOTS, 0:n, :],
                                          ps[:, 4 + q % 2, 0:P * n].rearrange("p (n t) -> p n t", n=n),
                                          obias[:, GP * q:GP * q + n].unsqueeze(2).to_broadcast([P, n, P]),
                                          add).then_inc(s_oev, 1)

            dve.memset(zr[:, 0, :, 3 * HR:KR], 1.0).then_inc(s_one, 1)
            for g in range(NG):
                toeplitz(0, g)
            with dve.Fori(0, NCHUNK) as j:
                chunk(j, False)
            chunk(NCHUNK, True)


_NAMES = ["log_dt", "log_A_real", "A_imag", "C_re", "C_im", "Dskip", "Wout", "bout", "w0", "b0", "w1", "b1",
          "Wg", "bg", "Wi", "bi", "Wc", "bc"]


def kernel(**inputs):
    import numpy as _np
    import concourse.bacc as _bacc
    from concourse import mybir as _mybir
    from concourse.bass_utils import run_bass_kernel_spmd as _run

    nc = _bacc.Bacc("TRN2", target_bir_lowering=False, num_devices=1)
    arrays, args = {}, []
    for name in ["x"] + ["L0_conv_" + n for n in _NAMES]:
        a = _np.ascontiguousarray(inputs[name])
        arrays[f"in_{name}_dram"] = a
        args.append(nc.dram_tensor(f"in_{name}_dram", a.shape, _mybir.dt.from_np(a.dtype),
                                   kind="ExternalInput").ap())
    out = nc.dram_tensor("out_dram", (B, C, F, T), F32, kind="ExternalOutput").ap()
    conv_seq_program(nc, *args, out)
    r = _run(nc, [arrays], core_ids=[0])
    return r.results[0]["out_dram"]
```
